# Optimizing a Trainium2 kernel written in Bass

```python
import numpy as np
import jax
import jax.numpy as jnp

def _softmax(x, axis=-1):
    return jax.nn.softmax(x, axis=axis)

def _gelu(x):
    return jax.nn.gelu(x, approximate=True)

def _silu(x):
    return jax.nn.silu(x)

def _sigmoid(x):
    return jax.nn.sigmoid(x)

def _layernorm(x, axis=-1, eps=1e-05):
    m = jnp.mean(x, axis=axis, keepdims=True)
    v = jnp.var(x, axis=axis, keepdims=True)
    return (x - m) / jnp.sqrt(v + eps)

def _scatter_add(tgt, idx, src, axis=0):
    return tgt.at[idx].add(src)

def _segment_sum(src, seg, n):
    return jax.ops.segment_sum(src, seg, n)
kernel_name = 'mk_adaln_d1_jaxref_r8_bed3bb'

def setup_inputs(seed: int=0):
    np.random.seed(seed)
    _w = jnp.asarray

    def _L0_attn_setup():
        import math
        import jax, jax.numpy as jnp
        import numpy as np
        B, S, D, H = (2, 256, 128, 16)
        HD = D // H
        key = jax.random.key(seed)
        k1, k2, k3 = jax.random.split(key, 3)
        h = jax.random.normal(k1, (B, S, D), dtype=jnp.float32)
        Wqvk = jax.random.normal(k2, (D, 3 * D), dtype=jnp.float32) * (1.0 / math.sqrt(D))
        Wo = jax.random.normal(k3, (D, D), dtype=jnp.float32) * (1.0 / math.sqrt(D))
        return {'h': h, 'Wqvk': Wqvk, 'Wo': Wo}
    _L0_attn_in = _L0_attn_setup()

    def _L0_ffn_setup():
        import jax, jax.numpy as jnp
        import numpy as np
        B, S, D = (2, 256, 128)
        E, H, K = (8, 704, 2)
        N_RESERVED = 4
        key = jax.random.key(seed)
        ks = jax.random.split(key, 5)
        scale = 0.02
        x = jax.random.normal(ks[0], (B, S, D), dtype=jnp.float32)
        gate_w = jax.random.normal(ks[1], (E, D), dtype=jnp.float32) * scale
        w1 = jax.random.normal(ks[2], (E, D, H), dtype=jnp.float32) * scale
        w3 = jax.random.normal(ks[3], (E, D, H), dtype=jnp.float32) * scale
        w2 = jax.random.normal(ks[4], (E, H, D), dtype=jnp.float32) * scale
        return {'x': x, 'gate_w': gate_w, 'w1': w1, 'w2': w2, 'w3': w3}
    _L0_ffn_in = _L0_ffn_setup()
    _L0_c = _w((lambda *s: np.random.randn(*s).astype(np.float32) * 0.05)(8, 128))
    _L0_wmod = _w((lambda *s: np.random.randn(*s).astype(np.float32) * 0.05)(128, 6 * 128) * 128 ** (-0.5))
    _d = {'L0_attn_h': _L0_attn_in['h'], 'L0_attn_Wqvk': _L0_attn_in['Wqvk'], 'L0_attn_Wo': _L0_attn_in['Wo'], 'L0_ffn_gate_w': _L0_ffn_in['gate_w'], 'L0_ffn_w1': _L0_ffn_in['w1'], 'L0_ffn_w2': _L0_ffn_in['w2'], 'L0_ffn_w3': _L0_ffn_in['w3'], 'L0_c': _L0_c, 'L0_wmod': _L0_wmod}
    _x0 = _d['L0_attn_h']
    _d['L0_attn_h'] = jax.random.normal(jax.random.fold_in(jax.random.key(seed), 1), (8, 256, 128), dtype=_x0.dtype)
    del _x0
    return _d

def reference(L0_attn_h, L0_attn_Wqvk, L0_attn_Wo, L0_ffn_gate_w, L0_ffn_w1, L0_ffn_w2, L0_ffn_w3, L0_c, L0_wmod):

    def _L0_attn_ref(h, Wqvk, Wo):
        import math
        import jax, jax.numpy as jnp
        import numpy as np
        B, S, D, H = (2, 256, 128, 16)
        HD = D // H
        b, s, d = h.shape
        qvk = (h @ Wqvk).reshape(b, s, 3, H, HD)
        q, v, k = (qvk[:, :, 0], qvk[:, :, 1], qvk[:, :, 2])
        scores = jnp.einsum('bshi,bthi->bsth', q, k)
        mask = jnp.where(jnp.arange(s)[None, :] > jnp.arange(s)[:, None], jnp.float32(-jnp.inf), jnp.float32(0.0))
        scores = scores + mask[None, :, :, None]
        scores = scores / math.sqrt(d)
        weights = jax.nn.softmax(scores, axis=2)
        wv = jnp.einsum('bsth,bthi->bshi', weights, v).reshape(b, s, d)
        return wv @ Wo

    def _L0_ffn_ref(x, gate_w, w1, w2, w3):
        import jax, jax.numpy as jnp
        import numpy as np
        B, S, D = (2, 256, 128)
        E, H, K = (8, 704, 2)
        N_RESERVED = 4
        b, s, d = x.shape
        T = b * s
        xf = x.reshape(T, d)
        logits = xf @ gate_w.T
        expert_ids = jnp.arange(E)
        logits = jnp.where(expert_ids[None, :] >= E - N_RESERVED, -jnp.inf, logits)
        weights = jax.nn.softmax(logits, axis=-1)
        top_w, top_idx = jax.lax.top_k(weights, K)
        top_w = top_w / jnp.sum(top_w, axis=-1, keepdims=True)
        cw = jnp.zeros((T, E), dtype=x.dtype).at[jnp.arange(T)[:, None], top_idx].add(top_w)
        h = jax.nn.silu(jnp.einsum('td,edh->teh', xf, w1)) * jnp.einsum('td,edh->teh', xf, w3)
        y = jnp.einsum('teh,ehd->ted', h, w2)
        out = jnp.einsum('te,ted->td', cw, y)
        return out.reshape(b, s, d)
    x = L0_attn_h
    mod = (_silu(L0_c) @ L0_wmod).reshape(L0_c.shape[0], 6, 1, -1)
    sa, ca, ga, sb, cb, gb = (mod[:, 0], mod[:, 1], mod[:, 2], mod[:, 3], mod[:, 4], mod[:, 5])
    ga = (2 * (ga >= 0) - 1) * jnp.maximum(jnp.abs(ga), 0.25)
    gb = (2 * (gb >= 0) - 1) * jnp.maximum(jnp.abs(gb), 0.25)
    h = _layernorm(x, axis=-1) * (1 + ca) + sa
    x = x + ga * _L0_attn_ref(h, L0_attn_Wqvk, L0_attn_Wo)
    h = _layernorm(x, axis=-1) * (1 + cb) + sb
    x = x + gb * _L0_ffn_ref(h, L0_ffn_gate_w, L0_ffn_w1, L0_ffn_w2, L0_ffn_w3)
    return x

_drawn_inputs = setup_inputs


def setup_inputs(seed=0):
    import zlib

    import numpy as np

    out = dict(_drawn_inputs(seed))
    spreads = {}
    factors = {'L0_ffn_gate_w': 8.0, 'L0_ffn_w1': 8.0, 'L0_ffn_w2': 8.0, 'L0_ffn_w3': 8.0}
    for name, (base, spread) in spreads.items():
        noise = np.random.default_rng([zlib.crc32(name.encode()), seed]).standard_normal(out[name].shape)
        drawn = base * np.exp(spread * noise) if base else spread * noise
        out[name] = jnp.asarray(drawn.astype(out[name].dtype))
    for name, factor in factors.items():
        out[name] = (out[name] * factor).astype(out[name].dtype)
    return out
```

```python
import concourse.bass as bass
from concourse import mybir
from contextlib import ExitStack


def adaln_block_kernel(
    nc: bass.Bass,
    h: bass.AP,
    wqvk: bass.AP,
    wo: bass.AP,
    gate_w: bass.AP,
    w1: bass.AP,
    w2: bass.AP,
    w3: bass.AP,
    c: bass.AP,
    wmod: bass.AP,
    out: bass.AP,
):
    fp32, fp32r, bf16 = mybir.dt.float32, mybir.dt.float32r, mybir.dt.bfloat16
    ALU, ACT, AX = mybir.AluOpType, mybir.ActivationFunctionType, mybir.AxisListType

    NBATCH, SEQ, D = h.shape
    NMOD = wmod.shape[1] // D
    NEXP, _, HID = w1.shape
    OPEN = NEXP - 4
    HEADS = 16
    HD = D // HEADS
    SCORE_SCALE = float(D) ** -0.5
    LN_EPS = 1e-5
    GATE_FLOOR = 0.25
    MASKED = -1.0e30
    P = 128
    TILES = SEQ // P
    STRIP = 32
    GROUP = P // STRIP
    GROUPS = HEADS // GROUP
    REP = 3
    CHUNK = 512
    CB = CHUNK // SEQ
    NCHUNK = NBATCH // CB
    CT = CHUNK // P
    PAIRS = OPEN // 2
    FULL = HID // P
    HALF = HID - FULL * P
    assert 2 * HALF == P and SEQ == 2 * P
    UP = 2 * FULL + 1
    UNITS = PAIRS * UP

    def expert_of(n):
        return 0 if n < FULL else None if n == FULL else 1

    ctx = ExitStack()
    with ctx:
        def sb(name, shape, dt=fp32):
            return ctx.enter_context(nc.sbuf_tensor(name, shape, dt))

        def sem(name):
            return ctx.enter_context(nc.semaphore(name))

        x_sb = sb("x_sb", [P, NBATCH * TILES, D])
        wqvk_sb = sb("wqvk_sb", [P, 3 * D])
        wo_sb = sb("wo_sb", [P, D])
        c_sb = sb("c_sb", [NBATCH, D])
        gate_sb = sb("gate_sb", [OPEN, D])
        w2_sb = sb("w2_sb", [P, UNITS, D])
        ident = sb("ident", [P, P])
        ident_bf = sb("ident_bf", [P, P], bf16)
        causal_bf = sb("causal_bf", [P, 2, P], bf16)
        minus_half = sb("minus_half", [P, TILES])
        sel = sb("sel", [2 * OPEN, OPEN + PAIRS, P], fp32r)
        before = sb("before", [P, OPEN, OPEN])
        wqk_hi = sb("wqk_hi", [P, 2, GROUPS * P], fp32r)
        wqk_lo = sb("wqk_lo", [P, 2, GROUPS * P], fp32r)
        row_tmp = sb("row_tmp", [P, 2])
        low_q = sb("low_q", [P, 1])
        low_k = sb("low_k", [P, 1])
        minus_row = sb("minus_row", [P, GROUPS])
        cT = sb("cT", [P, NBATCH])
        gate_wT = sb("gate_wT", [P, OPEN])
        mod = sb("mod", [P, NMOD, NBATCH])
        wo_gated = sb("wo_gated", [P, NBATCH, D])
        w1_hi = sb("w1_hi", [P, UNITS, P], fp32r)
        w1_lo = sb("w1_lo", [P, UNITS, P], fp32r)
        w3_hi = sb("w3_hi", [P, UNITS, P], fp32r)
        w3_lo = sb("w3_lo", [P, UNITS, P], fp32r)
        stats = sb("stats", [P, TILES, 6])
        mv = sb("mv", [P, TILES, 2])
        veps = sb("veps", [P, TILES])
        rstd = sb("rstd", [P, TILES])
        xn = sb("xn", [P, TILES, D])
        hT = sb("hT", [P, SEQ])
        hT_hi = sb("hT_hi", [P, SEQ], fp32r)
        hT_lo = sb("hT_lo", [P, SEQ], fp32r)
        cut = sb("cut", [P, 2, GROUPS, SEQ], fp32r)
        q_rows = sb("q_rows", [P, GROUPS, SEQ], fp32r)
        k_rows = sb("k_rows", [P, GROUPS, SEQ], fp32r)
        q_max = sb("q_max", [P, GROUPS, SEQ], fp32r)
        v_ones = sb("v_ones", [P, TILES, HEADS, STRIP])
        peak = sb("peak", [P, TILES, GROUP, STRIP])
        probs0 = sb("probs0", [P, 2, GROUP, SEQ])
        probs1 = sb("probs1", [P, 2, GROUP, P])
        oT = sb("oT", [P, GROUPS, SEQ])
        rden = sb("rden", [P, TILES, HEADS])
        attn = sb("attn", [P, TILES, HEADS, HD])
        attnT = sb("attnT", [P, SEQ])
        wqk_f = probs1[:].rearrange("p i g s -> p i (g s)")
        c_rows = oT[:].rearrange("p g s -> p (g s)").rearrange("p (b n) -> p b n", n=P)
        gsign = probs0[:, 0, :, :].rearrange("p g s -> p (g s)").rearrange("p (b d) -> p b d", d=D)
        gabs = probs0[:, 1, :, :].rearrange("p g s -> p (g s)").rearrange("p (b d) -> p b d", d=D)
        lmax = sb("lmax", [P, TILES])
        lshift = sb("lshift", [P, TILES, OPEN])
        prob = sb("prob", [P, TILES, OPEN])
        above = sb("above", [P, TILES, OPEN, OPEN])
        same = sb("same", [P, TILES, OPEN, OPEN])
        rank = sb("rank", [P, TILES, OPEN])
        kept = sb("kept", [P, TILES, OPEN])
        ksum = sb("ksum", [P, TILES])
        krec = sb("krec", [P, TILES])
        share = sb("share", [P, TILES, OPEN])
        share_cut = sb("share_cut", [P, TILES, 2 * OPEN], fp32r)
        x1 = sb("x1", [P, NBATCH * TILES, D])
        h2 = sb("h2", [P, SEQ])
        h2T = sb("h2T", [P, NBATCH * SEQ])
        h2_hi = sb("h2_hi", [P, NBATCH * SEQ], fp32r)
        h2_lo = sb("h2_lo", [P, NBATCH * SEQ], fp32r)
        shareT = sb("shareT", [2 * OPEN, NBATCH * SEQ], fp32r)
        xw = sb("xw", [P, CHUNK])
        xw_hi = sb("xw_hi", [P, 2, CHUNK], fp32r)
        xw_lo = sb("xw_lo", [P, 2, CHUNK], fp32r)
        pair_share = sb("pair_share", [P, CHUNK])
        work = sb("work", [P, 7, CHUNK])
        th, glu, hid = work[:, 0:2, :], work[:, 2:4, :], work[:, 4:7, :]
        hid_m = sb("hid_m", [P, CHUNK])
        yT = sb("yT", [P, CHUNK])
        y_out = sb("y_out", [P, CT, D])
        w_raw = work[:].rearrange("p n c -> p (n c)")[:, 0:UNITS * P].rearrange("p (u f) -> p u f", f=P)
        wmod_sb = h2T[:, 0:NMOD * D]
        sel_f = x1[0:2 * OPEN, 0:OPEN + PAIRS, :]
        c_exp, c_rec, c_silu = (x1[0:NBATCH, OPEN + PAIRS + n, :] for n in range(3))

        A = [ctx.enter_context(nc.psum_tensor(f"A{i}", [P, 2 * CHUNK], fp32)) for i in range(2)]
        T = ctx.enter_context(nc.psum_tensor("T", [P, CHUNK], fp32))
        G = ctx.enter_context(nc.psum_tensor("G", [P, CHUNK], fp32))
        U = ctx.enter_context(nc.psum_tensor("U", [P, CHUNK], fp32))
        Y = ctx.enter_context(nc.psum_tensor("Y", [P, CHUNK], fp32))

        x_in = sem("x_in")
        attn_w_in = sem("attn_w_in")
        mod_in = sem("mod_in")
        w1_in = sem("w1_in")
        w3_in = sem("w3_in")
        w2_in = sem("w2_in")
        pool_const = sem("pool_const")
        consts = sem("consts")
        wqk_step = sem("wqk_step")
        wqk_ready = sem("wqk_ready")
        setup_dve = sem("setup_dve")
        setup_pe = sem("setup_pe")
        setup_act = sem("setup_act")
        w_cut_hi = sem("w_cut_hi")
        w_cut = sem("w_cut")
        a_written = sem("a_written")
        a_read = sem("a_read")
        t_written = sem("t_written")
        t_read = sem("t_read")
        var_ready = sem("var_ready")
        rstd_ready = sem("rstd_ready")
        xn_ready = sem("xn_ready")
        hi_ready = sem("hi_ready")
        lo_ready = sem("lo_ready")
        cut_ready = sem("cut_ready")
        masked = sem("masked")
        prob_ready = sem("prob_ready")
        share_ready = sem("share_ready")
        dve_step = sem("dve_step")
        h2_kept = sem("h2_kept")
        xw_hi_ready = sem("xw_hi_ready")
        xw_cut = sem("xw_cut")
        g_written = sem("g_written")
        u_written = sem("u_written")
        tanh_done = sem("tanh_done")
        glu_done = sem("glu_done")
        u_read = sem("u_read")
        scaled = sem("scaled")
        down_done = sem("down_done")
        y_read = sem("y_read")
        out_sent = sem("out_sent")
        out_free = sem("out_free")
        waits_apart = sem("waits_apart")

        SETUP = 1
        N_A, N_T = 3 + 4 * GROUPS, 8 + GROUPS
        A_Q, A_K, A_S, A_E, A_O = 0, 1, 2, 2 + 2 * GROUPS, 2 + 4 * GROUPS
        (T_XN, T_V, T_MAX), T_PV = range(3), 3
        T_ATTN, T_WO, T_H2, T_LOGIT, T_SHARE = range(3 + GROUPS, 8 + GROUPS)
        N_TC = OPEN + PAIRS + 1
        T_END = N_T * NBATCH

        block = ctx.enter_context(nc.Block())

        def two_heads(n):
            return A[n % 2][:].rearrange("p (h i t) -> p h i t", h=2, i=TILES)

        def wait_apart(eng, s, value):
            eng.wait_ge(s, value)
            eng.sem_inc(waits_apart, 1)

        def unit_rows(w, raw, eng, s):
            n = 0
            for pair in range(PAIRS):
                e, u = 2 * pair, pair * UP
                flat = raw[:, u:u + UP, :].rearrange("p u f -> p (u f)")
                eng.dma_start(flat[:, 0:HID], w[e, :, :]).then_inc(s, 16)
                eng.dma_start(flat[:, HID:HID + HALF], w[e + 1, :, FULL * P:HID]).then_inc(s, 16)
                eng.dma_start(flat[:, HID + HALF:2 * HID], w[e + 1, :, 0:FULL * P]).then_inc(s, 16)
                n += 48
            return n
        W_IN = 48 * PAIRS

        @block.sync
        def _(sp):
            sp.dma_start(x_sb[:, 0:TILES, :],
                         h[0, :, :].rearrange("(t p) d -> p t d", p=P)).then_inc(x_in, 16)
            sp.dma_start(wqvk_sb[:], wqvk).then_inc(attn_w_in, 16)
            sp.dma_start(wo_sb[:], wo).then_inc(attn_w_in, 16)
            sp.dma_start(x_sb[:, TILES:, :], h[1:, :, :].rearrange("b (t p) d -> p (b t) d", p=P)
                         ).then_inc(x_in, 16)
            unit_rows(w1, w_raw, sp, w1_in)
            for pair in range(PAIRS):
                e, u = 2 * pair, pair * UP
                sp.dma_start(w2_sb[:, u:u + FULL, :],
                             w2[e, 0:FULL * P, :].rearrange("(u p) d -> p u d", p=P)).then_inc(w2_in, 16)
                sp.dma_start(w2_sb[0:HALF, u + FULL, :], w2[e, FULL * P:HID, :]).then_inc(w2_in, 16)
                sp.dma_start(w2_sb[HALF:P, u + FULL, :], w2[e + 1, FULL * P:HID, :]).then_inc(w2_in, 16)
                sp.dma_start(w2_sb[:, u + FULL + 1:u + UP, :],
                             w2[e + 1, 0:FULL * P, :].rearrange("(u p) d -> p u d", p=P)).then_inc(w2_in, 16)
            sp.wait_ge(w_cut, 1)
            unit_rows(w3, w_raw, sp, w3_in)
            sp.sem_inc(out_free, 1)
            with sp.Fori(0, NCHUNK) as ch:
                sp.wait_ge(t_read, SETUP + T_END + ch * N_TC + N_TC)
                sp.dma_start(out[bass.ds(ch * CB, CB), :, :].rearrange("b (t p) d -> p (b t) d", p=P),
                             y_out[:]).then_inc(out_sent, 16)
                sp.wait_ge(out_sent, 16 * ch + 16)
                sp.sem_inc(out_free, 1)

        @block.gpsimd
        def _(pool):
            nc.gpsimd.memset(ident[:], 0.0).then_inc(pool_const, 1)
            nc.gpsimd.memset(causal_bf[:], 0.0).then_inc(pool_const, 1)
            nc.gpsimd.memset(sel_f, 0.0).then_inc(pool_const, 1)
            nc.gpsimd.memset(before[:], 1.0).then_inc(pool_const, 1)
            nc.gpsimd.memset(minus_half[:], -0.5).then_inc(consts, 1)
            pool.wait_ge(pool_const, 4)
            nc.gpsimd.affine_select(out=ident[:], in_=ident[:], compare_op=ALU.not_equal, fill=1.0, base=0,
                                    pattern=[[-1, P]], channel_multiplier=1).then_inc(consts, 1)
            nc.gpsimd.affine_select(out=causal_bf[:], in_=causal_bf[:], compare_op=ALU.is_ge, fill=MASKED,
                                    base=0, pattern=[[0, 2], [-1, P]], channel_multiplier=1).then_inc(consts, 1)
            nc.gpsimd.affine_select(out=before[:], in_=before[:], compare_op=ALU.is_ge, fill=0.0, base=-1,
                                    pattern=[[1, OPEN], [-1, OPEN]], channel_multiplier=0).then_inc(consts, 1)
            for n, base in enumerate((0, -OPEN)):
                if n:
                    pool.wait_ge(pool_const, 6)
                nc.gpsimd.affine_select(out=sel_f[:, 0:OPEN, :], in_=sel_f[:, 0:OPEN, :],
                                        compare_op=ALU.not_equal, fill=1.0, base=base,
                                        pattern=[[-1, OPEN], [0, P]], channel_multiplier=1
                                        ).then_inc(pool_const, 1)
                halves = sel_f[:, OPEN:, :].rearrange("p m (s f) -> p m s f", s=2)
                nc.gpsimd.affine_select(out=halves, in_=halves, compare_op=ALU.not_equal, fill=1.0,
                                        base=base, pattern=[[-2, PAIRS], [-1, 2], [0, HALF]],
                                        channel_multiplier=1).then_inc(pool_const, 1)
            with pool.Fori(0, NBATCH) as b:
                pool.wait_ge(var_ready, b * 2 + 1)
                nc.gpsimd.tensor_tensor(rstd[:], veps[:], minus_half[:], ALU.pow).then_inc(rstd_ready, 1)
                for g in range(GROUPS):
                    wait_apart(pool, a_read, SETUP + b * N_A + A_E + 2 * g + 2)
                    for pr in (probs0, probs1):
                        part = pr[:, g % 2, :, 0:P]
                        nc.gpsimd.affine_select(out=part, in_=part, compare_op=ALU.is_ge, fill=0.0, base=0,
                                                pattern=[[0, GROUP], [1, P]], channel_multiplier=-1
                                                ).then_inc(masked, 1)
                pool.wait_ge(var_ready, b * 2 + 2)
                nc.gpsimd.tensor_tensor(rstd[:], veps[:], minus_half[:], ALU.pow).then_inc(rstd_ready, 1)
                pool.wait_ge(t_read, SETUP + b * N_T + T_H2 + 1)
                nc.gpsimd.tensor_copy(h2T[:, bass.ds(b * SEQ, SEQ)], h2[:]).then_inc(h2_kept, 1)

        @block.scalar
        def _(act):
            act.dma_start(c_sb[:], c).then_inc(mod_in, 16)
            act.dma_start(gate_sb[:], gate_w[0:OPEN, :]).then_inc(mod_in, 16)
            act.dma_start(wmod_sb, wmod).then_inc(mod_in, 16)
            act.wait_ge(mod_in, 48)
            nc.scalar.activation(c_exp, c_sb[:], ACT.Exp, scale=-1.0).then_inc(setup_act, 1)
            for n, (raw, hi, s) in enumerate(((w_raw, w1_hi, w1_in), (w_raw, w3_hi, w3_in))):
                act.wait_ge(s, W_IN)
                nc.scalar.activation(hi[:], raw, ACT.Copy).then_inc(w_cut_hi, 1)
            with act.Fori(0, NBATCH) as b:
                act.wait_ge(t_read, SETUP + b * N_T + T_XN + 1)
                nc.scalar.activation(hT_hi[:], hT[:], ACT.Copy).then_inc(hi_ready, 1)
                act.wait_ge(a_written, b * N_A + A_Q + 1)
                nc.scalar.activation(cut[:, 0, :, :], A[0][:].rearrange("p (g s) -> p g s", g=GROUPS),
                                     ACT.Copy).then_inc(cut_ready, 1)
                act.wait_ge(a_written, b * N_A + A_K + 1)
                for g in range(GROUPS):
                    last = nc.scalar.activation(cut[:, 1, g, :], A[1][:, g * SEQ:(g + 1) * SEQ], ACT.Identity,
                                                bias=minus_row[:, g:g + 1])
                last.then_inc(cut_ready, 1)
                for g in range(GROUPS):
                    for hp in range(2):
                        n = A_E + 2 * g + hp
                        act.wait_ge(a_written, b * N_A + n + 1)
                        if g >= 2 and hp == 0:
                            act.wait_ge(t_written, b * N_T + T_PV + g - 1)
                        s, heads = two_heads(n), slice(2 * hp, 2 * hp + 2)
                        nc.scalar.activation(probs0[:, g % 2, heads, :], s[:, :, 0, :], ACT.Exp,
                                             scale=SCORE_SCALE)
                        nc.scalar.activation(probs1[:, g % 2, heads, :], s[:, :, 1, P:SEQ], ACT.Exp,
                                             scale=SCORE_SCALE).then_inc(a_read, 1)
                act.wait_ge(t_written, b * N_T + T_ATTN + 1)
                nc.scalar.activation(attnT[:], T[:, 0:SEQ], ACT.Copy).then_inc(t_read, 1)
                act.wait_ge(t_read, SETUP + b * N_T + T_H2 + 1)
                nc.scalar.activation(h2_hi[:, bass.ds(b * SEQ, SEQ)], h2[:], ACT.Copy).then_inc(hi_ready, 1)
                act.wait_ge(t_read, SETUP + b * N_T + T_LOGIT + 1)
                nc.scalar.activation(prob[:], lshift[:], ACT.Exp).then_inc(prob_ready, 1)

            with act.Fori(0, NCHUNK) as ch:
                def round_xw(e):
                    pair, s = divmod(e, 2)
                    act.wait_ge(t_read, SETUP + ch * N_TC + T_END + 3 * pair + s + 1)
                    act.wait_ge(u_written, SETUP + ch * UNITS + (pair * UP if s or not pair else FULL))
                    nc.scalar.activation(xw_hi[:, e % 2, :], xw[:], ACT.Copy).then_inc(xw_hi_ready, 1)

                for pair in range(PAIRS):
                    for e in (2 * pair, 2 * pair + 1):
                        round_xw(e)
                    act.wait_ge(t_written, ch * N_TC + T_END + 3 * pair + 3)
                    nc.scalar.activation(pair_share[:], T[:], ACT.Copy).then_inc(t_read, 1)
                    for n in range(UP):
                        u = pair * UP + n
                        act.wait_ge(g_written, ch * UNITS + u + 1)
                        if u >= 2:
                            act.wait_ge(glu_done, SETUP + ch * UNITS + u - 1)
                        nc.scalar.activation(th[:, u % 2, :], G[:], ACT.Tanh, scale=0.5).then_inc(tanh_done, 1)

        @block.tensor
        def _(pe):
            def cut_product(dst, w_hi, w_lo, x_hi, x_lo):
                nc.tensor.matmul(dst, w_hi, x_hi, start=True, stop=False)
                nc.tensor.matmul(dst, w_hi, x_lo, start=False, stop=False)
                return nc.tensor.matmul(dst, w_lo, x_hi, start=False, stop=True)

            pe.wait_ge(consts, 4)
            pe.wait_ge(mod_in, 48)
            nc.tensor.transpose(T[:, 0:OPEN], gate_sb[:], ident[0:OPEN, 0:OPEN]).then_inc(setup_pe, 1)
            pe.wait_ge(setup_dve, 3)
            nc.tensor.transpose(G[:, 0:NBATCH], c_silu, ident[0:NBATCH, 0:NBATCH]).then_inc(setup_pe, 1)
            pe.wait_ge(setup_dve, 4)
            for m in range(NMOD):
                last = nc.tensor.matmul(U[:, m * NBATCH:(m + 1) * NBATCH], wmod_sb[:, m * D:(m + 1) * D],
                                        cT[:], start=True, stop=True)
            last.then_inc(u_written, 1)
            for b in range(NBATCH):
                last = nc.tensor.matmul(A[0][:, b * D:(b + 1) * D], c_rows[:, b, :], wmod_sb[:, 2 * D:3 * D],
                                        start=True, stop=True)
            last.then_inc(setup_pe, 1)

            pe.wait_ge(wqk_ready, 1)
            pe.wait_ge(attn_w_in, 32)
            with pe.Fori(0, NBATCH) as b:
                def t_free(n):
                    pe.wait_ge(t_read, SETUP + b * N_T + n)

                def a_free(n):
                    pe.wait_ge(a_read, SETUP + b * N_A + max(n - 1, 0))

                pe.wait_ge(xn_ready, b * 2 + 1)
                t_free(T_XN)
                for i in range(TILES):
                    last = nc.tensor.transpose(T[:, i * P:(i + 1) * P], xn[:, i, :], ident[:])
                last.then_inc(t_written, 1)
                pe.wait_ge(lo_ready, b * 2 + 1)
                for n in (A_Q, A_K):
                    a_free(n)
                    for g in range(GROUPS):
                        cols = slice(g * P, (g + 1) * P)
                        last = cut_product(A[n][:, g * SEQ:(g + 1) * SEQ], wqk_hi[:, n, cols],
                                           wqk_lo[:, n, cols], hT_hi[:], hT_lo[:])
                    last.then_inc(a_written, 1)
                t_free(T_V)
                for i in range(TILES):
                    last = nc.tensor.matmul(T[:, i * P:(i + 1) * P], hT[:, i * P:(i + 1) * P],
                                            wqvk_sb[:, D:2 * D], start=True, stop=True)
                last.then_inc(t_written, 1)
                for g in range(GROUPS):
                    for hp in range(2):
                        n = A_S + 2 * g + hp
                        a_free(n)
                        if n == A_S:
                            pe.wait_ge(a_read, SETUP + b * N_A + 2)
                        dst = two_heads(n)
                        for k in range(2):
                            blocks = dst[:, k, :, :].rearrange("p i t -> p (i t)").rearrange(
                                "p (n t) -> p n t", t=P)
                            nc.tensor.matmul(blocks[:, 0:4:3, :], ident_bf[:],
                                             causal_bf[:], start=True, stop=True)
                        for i in range(TILES):
                            for k in range(2):
                                rows = slice((2 * hp + k) * STRIP, (2 * hp + k + 1) * STRIP)
                                last = nc.tensor.matmul(dst[:, k, i, :], q_rows[rows, g, i * P:(i + 1) * P],
                                                        k_rows[rows, g, :], start=False, stop=True,
                                                        skip_group_check=True)
                        last.then_inc(a_written, 1)
                pe.wait_ge(a_read, SETUP + b * N_A + A_E)
                t_free(T_MAX)
                for i in range(TILES):
                    last = nc.tensor.transpose(T[:, i * P:(i + 1) * P],
                                               peak[:, i, :, :].rearrange("p j r -> p (j r)"), ident[:])
                last.then_inc(t_written, 1)

                def scores(g):
                    for hp in range(2):
                        n = A_E + 2 * g + hp
                        a_free(n)
                        dst = two_heads(n)
                        for i in range(TILES):
                            for k in range(2):
                                rows = slice((2 * hp + k) * STRIP, (2 * hp + k + 1) * STRIP)
                                last = nc.tensor.matmul(dst[:, k, i, :], k_rows[rows, g, i * P:(i + 1) * P],
                                                        q_max[rows, g, :], start=i == 0, stop=True,
                                                        skip_group_check=True)
                        last.then_inc(a_written, 1)

                def weigh(g):
                    t_free(T_PV + g)
                    pe.wait_ge(masked, b * 2 * GROUPS + 2 * g + 2)
                    for j in range(GROUP):
                        nc.tensor.matmul(T[j * STRIP:(j + 1) * STRIP, 0:SEQ], v_ones[:, 0, g * GROUP + j, :],
                                         probs0[:, g % 2, j, :], start=True, stop=False)
                    for j in range(GROUP):
                        last = nc.tensor.matmul(T[j * STRIP:(j + 1) * STRIP, P:SEQ],
                                                v_ones[:, 1, g * GROUP + j, :], probs1[:, g % 2, j, :],
                                                start=False, stop=True)
                    last.then_inc(t_written, 1)

                t_free(T_PV)
                for g in range(GROUPS):
                    scores(g)
                    if g:
                        weigh(g - 1)
                weigh(GROUPS - 1)
                a_free(A_O)
                t_free(T_ATTN)
                for i in range(TILES):
                    for g in range(GROUPS):
                        last = nc.tensor.transpose(A[0][:, i * CHUNK + g * P:i * CHUNK + (g + 1) * P],
                                                   oT[:, g, i * P:(i + 1) * P], ident[:])
                last.then_inc(a_written, 1)
                pe.wait_ge(a_read, SETUP + b * N_A + N_A)
                for i in range(TILES):
                    last = nc.tensor.transpose(T[:, i * P:(i + 1) * P],
                                               attn[:, i, :, :].rearrange("p h d -> p (h d)"), ident[:])
                last.then_inc(t_written, 1)
                t_free(T_WO)
                for i in range(TILES):
                    last = nc.tensor.matmul(T[:, i * D:(i + 1) * D], attnT[:, i * P:(i + 1) * P],
                                            wo_gated[:, bass.ds(b, 1), :].rearrange("p a d -> p (a d)"),
                                            start=True, stop=True)
                last.then_inc(t_written, 1)
                pe.wait_ge(xn_ready, b * 2 + 2)
                for i in range(TILES):
                    last = nc.tensor.transpose(T[:, i * P:(i + 1) * P], xn[:, i, :], ident[:])
                last.then_inc(t_written, 1)
                t_free(T_LOGIT)
                for i in range(TILES):
                    last = nc.tensor.matmul(T[:, i * OPEN:(i + 1) * OPEN], h2[:, i * P:(i + 1) * P],
                                            gate_wT[:], start=True, stop=True)
                last.then_inc(t_written, 1)
                pe.wait_ge(share_ready, b + 1)
                for i in range(TILES):
                    last = nc.tensor.transpose(T[0:2 * OPEN, i * P:(i + 1) * P],
                                               share_cut[:, i, :].bitcast(fp32), ident[:])
                last.then_inc(t_written, 1)

            pe.wait_ge(w_cut, 2)
            pe.wait_ge(w2_in, 64 * PAIRS)
            pe.wait_ge(lo_ready, 2 * NBATCH)
            with pe.Fori(0, NCHUNK) as ch:
                tokens = bass.ds(ch * CHUNK, CHUNK)

                def spread(slot, n):
                    wait_apart(pe, t_read, SETUP + ch * N_TC + T_END + n)
                    nc.tensor.matmul(T[:], sel[:, slot, :], shareT[:, tokens], start=True,
                                     stop=True).then_inc(t_written, 1)

                def down(u):
                    pe.wait_ge(u_read, SETUP + ch * UNITS + u + 1)
                    if u % UP == FULL:
                        pe.wait_ge(scaled, ch * PAIRS + u // UP + 1)
                    h_u = hid_m[:] if u % UP == FULL else hid[:, u % 3, :]
                    m = nc.tensor.matmul(Y[:], w2_sb[:, u, :], h_u, start=u == 0, stop=u == UNITS - 1)
                    m.then_inc(down_done, 1)

                for pair in range(PAIRS):
                    spread(2 * pair, 3 * pair)
                    spread(2 * pair + 1, 3 * pair + 1)
                    spread(OPEN + pair, 3 * pair + 2)
                    for n in range(UP):
                        u, s = pair * UP + n, expert_of(n)
                        pe.wait_ge(glu_done, SETUP + ch * UNITS + u)
                        cut_product(G[:], w1_hi[:, u, :], w1_lo[:, u, :], h2_hi[:, tokens],
                                    h2_lo[:, tokens]).then_inc(g_written, 1)
                        if n in (0, FULL + 1):
                            pe.wait_ge(xw_cut, ch * OPEN + 2 * pair + s + 1)
                        pe.wait_ge(u_read, SETUP + ch * UNITS + u)
                        xs = (h2_hi[:, tokens], h2_lo[:, tokens]) if s is None else \
                            (xw_hi[:, s, :], xw_lo[:, s, :])
                        last = cut_product(U[:], w3_hi[:, u, :], w3_lo[:, u, :], *xs)
                        last.then_inc(u_written, 1)
                        if u:
                            down(u - 1)
                down(UNITS - 1)
                pe.wait_ge(t_read, SETUP + ch * N_TC + T_END + N_TC - 1)
                pe.wait_ge(y_read, ch + 1)
                for i in range(CT):
                    last = nc.tensor.transpose(T[:, i * P:(i + 1) * P], yT[:, i * P:(i + 1) * P], ident[:])
                last.then_inc(t_written, 1)

        @block.vector
        def _(dve):
            done = [0]

            def setup(ins):
                done[0] += 1
                ins.then_inc(setup_dve, 1)
                dve.wait_ge(setup_dve, done[0])

            dve.wait_ge(setup_act, 1)
            setup(nc.vector.tensor_scalar_add(c_exp, c_exp, 1.0))
            setup(nc.vector.reciprocal(c_rec, c_exp))
            setup(nc.vector.tensor_tensor(c_silu, c_sb[:], c_rec, ALU.mult))
            dve.wait_ge(setup_pe, 1)
            nc.vector.tensor_copy(gate_wT[:], T[:, 0:OPEN]).then_inc(t_read, 1)
            dve.wait_ge(setup_pe, 2)
            nc.vector.tensor_copy(cT[:], G[:, 0:NBATCH]).then_inc(glu_done, 1)
            dve.wait_ge(glu_done, SETUP)
            setup(nc.vector.tensor_copy(c_rows, cT[:].unsqueeze(2).to_broadcast([P, NBATCH, P])))
            dve.wait_ge(u_written, SETUP)
            m_ps = U[:, 0:NMOD * NBATCH].rearrange("p (m b) -> p m b", m=NMOD)
            nc.vector.tensor_copy(mod[:, 0, :], m_ps[:, 0, :]).then_inc(u_read, 1)
            nc.vector.tensor_scalar_add(mod[:, 1, :], m_ps[:, 1, :], 1.0)
            nc.vector.tensor_copy(mod[:, 3, :], m_ps[:, 3, :])
            nc.vector.tensor_scalar_add(mod[:, 4, :], m_ps[:, 4, :], 1.0)
            def clamp(dst, g, sign, size):
                nc.vector.tensor_copy(size, g)
                setup(nc.vector.tensor_scalar(sign, g, 0.0, 2.0, ALU.is_ge, ALU.mult))
                setup(nc.vector.tensor_scalar_add(sign, sign, -1.0))
                setup(nc.vector.scalar_tensor_tensor(out=size, in0=size, scalar=-1.0, in1=size,
                                                     op0=ALU.mult, op1=ALU.max))
                setup(nc.vector.scalar_tensor_tensor(out=dst, in0=size, scalar=GATE_FLOOR, in1=sign,
                                                     op0=ALU.max, op1=ALU.mult))

            flat_sign, flat_size = (t.rearrange("p b d -> p (b d)") for t in (gsign, gabs))
            clamp(mod[:, 5, :], m_ps[:, 5, :], flat_sign[:, 0:NBATCH], flat_size[:, 0:NBATCH])
            dve.wait_ge(setup_pe, 3)
            dve.wait_ge(attn_w_in, 32)
            clamp(flat_size, A[0][:], flat_sign, flat_size)
            nc.vector.tensor_tensor(wo_gated[:], gabs, wo_sb[:].unsqueeze(1).to_broadcast([P, NBATCH, D]),
                                    ALU.mult).then_inc(a_read, 1)
            dve.wait_ge(consts, 4)
            nc.vector.tensor_copy(ident_bf[:], ident[:])
            nc.vector.memset(v_ones[:], 0.0).then_inc(wqk_step, 1)
            nc.vector.memset(peak[:], 0.0).then_inc(wqk_step, 1)
            nc.vector.memset(wqk_f, 0.0).then_inc(wqk_step, 1)
            dve.wait_ge(wqk_step, 3)
            for n, at in ((0, 0), (1, 2 * D)):
                dst = wqk_f[:, n, :].rearrange("p (h r) -> p h r", r=STRIP)
                for r in range(REP):
                    last = nc.vector.tensor_copy(dst[:, :, r * HD:(r + 1) * HD],
                                                 wqvk_sb[:, at:at + D].rearrange("p (h d) -> p h d", d=HD))
            last.then_inc(wqk_step, 1)
            nc.vector.memset(v_ones[:, :, :, HD:HD + 1], 1.0)
            id_rows = ident[:].rearrange("p (j r) -> p j r", r=STRIP)
            nc.vector.tensor_reduce(low_q[:], id_rows[:, :, 2 * HD:3 * HD], AX.XY, ALU.add, negate=True)
            nc.vector.tensor_reduce(row_tmp[:, 0:1], id_rows[:, :, HD:2 * HD], AX.XY, ALU.add)
            nc.vector.tensor_reduce(row_tmp[:, 1:2], id_rows[:, :, REP * HD:REP * HD + GROUPS], AX.XY, ALU.add)
            nc.vector.tensor_reduce(minus_row[:], id_rows[:, :, REP * HD:REP * HD + GROUPS].rearrange(
                "p j g -> p g j"), AX.X, ALU.add, negate=True)
            dve.wait_ge(pool_const, 8)
            nc.vector.tensor_copy(sel[:], sel_f).then_inc(wqk_step, 1)
            dve.wait_ge(wqk_step, 5)
            nc.vector.tensor_tensor(low_k[:], row_tmp[:, 1:2], row_tmp[:, 0:1], ALU.subtract)
            nc.vector.tensor_copy(wqk_hi[:], wqk_f).then_inc(wqk_step, 1)
            dve.wait_ge(wqk_step, 6)
            nc.vector.tensor_tensor(wqk_lo[:], wqk_f, wqk_hi[:].bitcast(fp32),
                                    ALU.subtract).then_inc(wqk_ready, 1)
            for n, (raw, hi, lo) in enumerate(((w_raw, w1_hi, w1_lo), (w_raw, w3_hi, w3_lo))):
                dve.wait_ge(w_cut_hi, n + 1)
                nc.vector.tensor_tensor(lo[:], raw, hi[:].bitcast(fp32), ALU.subtract).then_inc(w_cut, 1)

            dve.wait_ge(x_in, 32)
            STEPS = 15
            with dve.Fori(0, NBATCH) as b:
                step = [0]

                def then(ins):
                    step[0] += 1
                    ins.then_inc(dve_step, 1)
                    wait_apart(dve, dve_step, b * STEPS + step[0])

                def norm(src, k):
                    for i in range(TILES):
                        ins = nc.vector.bn_stats(stats[:, i, :], src[:, bass.ds(b * TILES + i, 1), :].rearrange(
                            "p a d -> p (a d)"))
                    then(ins)
                    for i in range(TILES):
                        ins = nc.vector.bn_aggr(mv[:, i, :], stats[:, i, :])
                    then(ins)
                    nc.vector.tensor_scalar_add(veps[:], mv[:, :, 1], LN_EPS).then_inc(var_ready, 1)
                    dve.wait_ge(rstd_ready, b * 2 + k + 1)
                    for i in range(TILES):
                        ins = nc.vector.tensor_scalar(
                            xn[:, i, :], src[:, bass.ds(b * TILES + i, 1), :].rearrange("p a d -> p (a d)"),
                            mv[:, i, 0:1], rstd[:, i:i + 1], ALU.subtract, ALU.mult)
                    ins.then_inc(xn_ready, 1)

                def t_wait(n):
                    dve.wait_ge(t_written, b * N_T + n + 1)

                norm(x_sb, 0)
                t_wait(T_XN)
                nc.vector.tensor_scalar(hT[:], T[:, 0:SEQ], mod[:, 1, bass.ds(b, 1)], mod[:, 0, bass.ds(b, 1)],
                                        ALU.mult, ALU.add).then_inc(t_read, 1)
                dve.wait_ge(hi_ready, b * 2 + 1)
                nc.vector.tensor_tensor(hT_lo[:], hT[:], hT_hi[:].bitcast(fp32), ALU.subtract)\
                    .then_inc(lo_ready, 1)
                dve.wait_ge(cut_ready, b * 2 + 1)
                nc.vector.scalar_tensor_tensor(
                    out=q_rows[:].rearrange("p g s -> p (g s)"),
                    in0=cut[:, 0, :, :].rearrange("p g s -> p (g s)").bitcast(fp32), scalar=low_q[:, 0:1],
                    in1=A[0][:], op0=ALU.mult, op1=ALU.add).then_inc(a_read, 1)
                dve.wait_ge(cut_ready, b * 2 + 2)
                nc.vector.scalar_tensor_tensor(
                    out=k_rows[:].rearrange("p g s -> p (g s)"),
                    in0=cut[:, 1, :, :].rearrange("p g s -> p (g s)").bitcast(fp32), scalar=low_k[:, 0:1],
                    in1=A[1][:], op0=ALU.mult, op1=ALU.add).then_inc(a_read, 1)
                t_wait(T_V)
                nc.vector.tensor_copy(v_ones[:, :, :, 0:HD].rearrange("p t h d -> p (t h) d"),
                                      T[:, 0:SEQ].rearrange("p (n d) -> p n d", d=HD)).then_inc(t_read, 1)
                for g in range(GROUPS):
                    for hp in range(2):
                        n = A_S + 2 * g + hp
                        dve.wait_ge(a_written, b * N_A + n + 1)
                        for i in range(TILES):
                            ins = nc.vector.reduce_max(peak[:, i, 2 * hp:2 * hp + 2, REP * HD + g],
                                                       two_heads(n)[:, :, i, 0:(i + 1) * P], AX.X)
                        ins.then_inc(a_read, 1)
                t_wait(T_MAX)
                nc.vector.tensor_tensor(q_max[:], q_rows[:].bitcast(fp32),
                                        T[:, 0:SEQ].unsqueeze(1).to_broadcast([P, GROUPS, SEQ]),
                                        ALU.add).then_inc(t_read, 1)
                for g in range(GROUPS):
                    t_wait(T_PV + g)
                    nc.vector.tensor_copy(oT[:, g, :], T[:, 0:SEQ]).then_inc(t_read, 1)
                dve.wait_ge(a_written, b * N_A + A_O + 1)
                sums = A[0][:].rearrange("p (t h r) -> p t h r", t=TILES, r=STRIP)
                then(nc.vector.reciprocal(rden[:], sums[:, :, :, HD]))
                nc.vector.tensor_tensor(attn[:], sums[:, :, :, 0:HD],
                                        rden[:].unsqueeze(3).to_broadcast([P, TILES, HEADS, HD]),
                                        ALU.mult).then_inc(a_read, 1)
                t_wait(T_WO)
                tiles = bass.ds(b * TILES, TILES)
                nc.vector.tensor_tensor(x1[:, tiles, :], x_sb[:, tiles, :],
                                        T[:, 0:SEQ].rearrange("p (t d) -> p t d", t=TILES),
                                        ALU.add).then_inc(t_read, 1)
                wait_apart(dve, t_read, SETUP + b * N_T + T_WO + 1)
                norm(x1, 1)
                t_wait(T_H2)
                nc.vector.tensor_scalar(h2[:], T[:, 0:SEQ], mod[:, 4, bass.ds(b, 1)], mod[:, 3, bass.ds(b, 1)],
                                        ALU.mult, ALU.add).then_inc(t_read, 1)
                dve.wait_ge(hi_ready, b * 2 + 2)
                nc.vector.tensor_tensor(h2_lo[:, bass.ds(b * SEQ, SEQ)], h2[:],
                                        h2_hi[:, bass.ds(b * SEQ, SEQ)].bitcast(fp32),
                                        ALU.subtract).then_inc(lo_ready, 1)
                t_wait(T_LOGIT)
                logits = T[:, 0:TILES * OPEN].rearrange("p (t e) -> p t e", e=OPEN)
                then(nc.vector.reduce_max(lmax[:], logits, AX.X))
                nc.vector.tensor_tensor(lshift[:], logits, lmax[:].unsqueeze(2).to_broadcast([P, TILES, OPEN]),
                                        ALU.subtract).then_inc(t_read, 1)
                dve.wait_ge(prob_ready, b + 1)
                square = [P, TILES, OPEN, OPEN]
                other = prob[:].unsqueeze(2).to_broadcast(square)
                own = prob[:].unsqueeze(3).to_broadcast(square)
                nc.vector.tensor_tensor(above[:], other, own, ALU.is_gt)
                then(nc.vector.tensor_tensor(same[:], other, own, ALU.is_equal))
                then(nc.vector.tensor_tensor(same[:], same[:], before[:].unsqueeze(1).to_broadcast(square),
                                             ALU.mult))
                then(nc.vector.tensor_tensor(above[:], above[:], same[:], ALU.add))
                then(nc.vector.reduce_sum(rank[:], above[:], AX.X))
                then(nc.vector.scalar_tensor_tensor(out=kept[:], in0=rank[:], scalar=2.0, in1=prob[:],
                                                    op0=ALU.is_lt, op1=ALU.mult))
                then(nc.vector.reduce_sum(ksum[:], kept[:], AX.X))
                then(nc.vector.reciprocal(krec[:], ksum[:]))
                then(nc.vector.scalar_tensor_tensor(out=share[:], in0=kept[:], scalar=0.5,
                                                    in1=krec[:].unsqueeze(2).to_broadcast([P, TILES, OPEN]),
                                                    op0=ALU.mult, op1=ALU.mult))
                then(nc.vector.tensor_copy(share_cut[:, :, 0:OPEN], share[:]))
                nc.vector.tensor_tensor(share_cut[:, :, OPEN:], share[:], share_cut[:, :, 0:OPEN].bitcast(fp32),
                                        ALU.subtract).then_inc(share_ready, 1)
                t_wait(T_SHARE)
                nc.vector.tensor_copy(shareT[:, bass.ds(b * SEQ, SEQ)], T[0:2 * OPEN, 0:SEQ]).then_inc(t_read, 1)
                assert step[0] == STEPS, step[0]

            dve.wait_ge(h2_kept, NBATCH)
            dve.wait_ge(t_read, SETUP + T_END)
            with dve.Fori(0, NCHUNK) as ch:
                tokens = bass.ds(ch * CHUNK, CHUNK)
                for pair in range(PAIRS):
                    for s in range(2):
                        e = 2 * pair + s
                        dve.wait_ge(t_written, ch * N_TC + T_END + 3 * pair + s + 1)
                        if e:
                            dve.wait_ge(xw_cut, ch * OPEN + e)
                        nc.vector.tensor_tensor(xw[:], h2T[:, tokens], T[:], ALU.mult).then_inc(t_read, 1)
                        dve.wait_ge(xw_hi_ready, ch * OPEN + e + 1)
                        nc.vector.tensor_tensor(xw_lo[:, s, :], xw[:], xw_hi[:, s, :].bitcast(fp32),
                                                ALU.subtract).then_inc(xw_cut, 1)
                    for n in range(UP):
                        u = pair * UP + n
                        dve.wait_ge(tanh_done, ch * UNITS + u + 1)
                        nc.vector.scalar_tensor_tensor(out=glu[:, u % 2, :], in0=th[:, u % 2, :], scalar=1.0,
                                                       in1=G[:], op0=ALU.add, op1=ALU.mult).then_inc(glu_done, 1)
                        dve.wait_ge(u_written, SETUP + ch * UNITS + u + 1)
                        dve.wait_ge(glu_done, SETUP + ch * UNITS + u + 1)
                        if u >= 3:
                            dve.wait_ge(down_done, ch * UNITS + u - 2)
                        nc.vector.tensor_tensor(hid[:, u % 3, :], glu[:, u % 2, :], U[:],
                                                ALU.mult).then_inc(u_read, 1)
                        if n == FULL:
                            dve.wait_ge(u_read, SETUP + ch * UNITS + u + 1)
                            dve.wait_ge(t_read, SETUP + ch * N_TC + T_END + 3 * pair + 3)
                            nc.vector.tensor_tensor(hid_m[:], hid[:, u % 3, :], pair_share[:],
                                                    ALU.mult).then_inc(scaled, 1)
                dve.wait_ge(down_done, ch * UNITS + UNITS)
                for k in range(CB):
                    ins = nc.vector.tensor_scalar(yT[:, k * SEQ:(k + 1) * SEQ], Y[:, k * SEQ:(k + 1) * SEQ],
                                                  mod[:, 5, bass.ds(ch * CB + k, 1)], None, ALU.mult)
                ins.then_inc(y_read, 1)
                dve.wait_ge(t_written, ch * N_TC + T_END + N_TC)
                dve.wait_ge(out_free, ch + 1)
                nc.vector.tensor_tensor(y_out[:], x1[:, bass.ds(ch * CT, CT), :],
                                        T[:].rearrange("p (t d) -> p t d", t=CT), ALU.add)\
                    .then_inc(t_read, 1)


_INS = ['L0_attn_h', 'L0_attn_Wqvk', 'L0_attn_Wo', 'L0_ffn_gate_w', 'L0_ffn_w1', 'L0_ffn_w2', 'L0_ffn_w3',
        'L0_c', 'L0_wmod']


def kernel(**inputs):
    import numpy as _np
    import concourse.bacc as _bacc
    from concourse import mybir as _mybir
    from concourse.bass_utils import run_bass_kernel_spmd as _run

    nc = _bacc.Bacc("TRN2", target_bir_lowering=False, num_devices=1)
    arrays, args = {}, []
    for name in _INS:
        a = _np.ascontiguousarray(inputs[name])
        arrays[f"in_{name}_dram"] = a
        args.append(nc.dram_tensor(f"in_{name}_dram", a.shape, _mybir.dt.from_np(a.dtype), kind="ExternalInput").ap())
    shape = inputs['L0_attn_h'].shape
    args.append(nc.dram_tensor("out_0_dram", shape, _mybir.dt.float32, kind="ExternalOutput").ap())
    adaln_block_kernel(nc, *args)
    r = _run(nc, [arrays], core_ids=[0])
    return r.results[0]["out_0_dram"]
```

```python
import concourse.bass as bass
from concourse import mybir
from contextlib import ExitStack


def adaln_block_kernel(
    nc: bass.Bass,
    h: bass.AP,
    wqvk: bass.AP,
    wo: bass.AP,
    gate_w: bass.AP,
    w1: bass.AP,
    w2: bass.AP,
    w3: bass.AP,
    c: bass.AP,
    wmod: bass.AP,
    out: bass.AP,
):
    fp32, fp32r, bf16 = mybir.dt.float32, mybir.dt.float32r, mybir.dt.bfloat16
    ALU, ACT, AX = mybir.AluOpType, mybir.ActivationFunctionType, mybir.AxisListType

    NBATCH, SEQ, D = h.shape
    NMOD = wmod.shape[1] // D
    NEXP, _, HID = w1.shape
    OPEN = NEXP - 4
    HEADS = 16
    HD = D // HEADS
    SCORE_SCALE = float(D) ** -0.5
    LN_EPS = 1e-5
    GATE_FLOOR = 0.25
    MASKED = -1.0e30
    P = 128
    TILES = SEQ // P
    STRIP = 32
    GROUP = P // STRIP
    GROUPS = HEADS // GROUP
    REP = 3
    BANK = 512
    PAIRS = OPEN // 2
    FULL = HID // P
    HALF = HID - FULL * P
    assert 2 * HALF == P and SEQ == 2 * P
    UP = 2 * FULL + 1
    UNITS = PAIRS * UP
    LAG = 2
    SLOTS = 4

    def expert_of(n):
        return 0 if n < FULL else None if n == FULL else 1

    ctx = ExitStack()
    with ctx:
        def sb(name, shape, dt=fp32):
            return ctx.enter_context(nc.sbuf_tensor(name, shape, dt))

        def sem(name):
            return ctx.enter_context(nc.semaphore(name))

        x_sb = sb("x_sb", [P, NBATCH * TILES, D])
        wqvk_sb = sb("wqvk_sb", [P, 3 * D])
        wo_sb = sb("wo_sb", [P, D])
        c_sb = sb("c_sb", [NBATCH, D])
        gate_sb = sb("gate_sb", [OPEN, D])
        ident = sb("ident", [P, P])
        ident_bf = sb("ident_bf", [P, P], bf16)
        causal_bf = sb("causal_bf", [P, 2, P], bf16)
        minus_half = sb("minus_half", [P, TILES])
        sel = sb("sel", [2 * OPEN, OPEN + PAIRS, P], fp32r)
        before = sb("before", [P, OPEN, OPEN])
        wqk_hi = sb("wqk_hi", [P, 2, GROUPS * P], fp32r)
        wqk_lo = sb("wqk_lo", [P, 2, GROUPS * P], fp32r)
        row_tmp = sb("row_tmp", [P, 2])
        low_q = sb("low_q", [P, 1])
        low_k = sb("low_k", [P, 1])
        minus_row = sb("minus_row", [P, GROUPS])
        cT = sb("cT", [P, NBATCH])
        gate_wT = sb("gate_wT", [P, OPEN])
        mod = sb("mod", [P, NMOD, NBATCH])
        wo_gated = sb("wo_gated", [P, NBATCH, D])
        w1_hi = sb("w1_hi", [P, UNITS, P], fp32r)
        w1_lo = sb("w1_lo", [P, UNITS, P], fp32r)
        w3_hi = sb("w3_hi", [P, UNITS, P], fp32r)
        w3_lo = sb("w3_lo", [P, UNITS, P], fp32r)
        w2_hi = sb("w2_hi", [P, UNITS, D], fp32r)
        w2_lo = sb("w2_lo", [P, UNITS, D], fp32r)
        stats = sb("stats", [P, 2, TILES, 6])
        mv = sb("mv", [P, 2, TILES, 2])
        veps = sb("veps", [P, 2, TILES])
        rstd = sb("rstd", [P, 2, TILES])
        xn = sb("xn", [P, 2, TILES, D])
        hT = sb("hT", [P, SEQ])
        hT_hi = sb("hT_hi", [P, SEQ], fp32r)
        hT_lo = sb("hT_lo", [P, SEQ], fp32r)
        cut = sb("cut", [P, 2, GROUPS, SEQ], fp32r)
        q_rows = sb("q_rows", [P, GROUPS, SEQ], fp32r)
        k_rows = sb("k_rows", [P, GROUPS, SEQ], fp32r)
        q_max = sb("q_max", [P, GROUPS, SEQ], fp32r)
        v_ones = sb("v_ones", [P, TILES, HEADS, STRIP])
        peak = sb("peak", [P, TILES, GROUP, STRIP])
        probs0 = sb("probs0", [P, 2, GROUP, SEQ])
        probs1 = sb("probs1", [P, 2, GROUP, P])
        oT = sb("oT", [P, GROUPS, SEQ])
        rden = sb("rden", [P, TILES, HEADS])
        attn = sb("attn", [P, TILES, HEADS, HD])
        attnT = sb("attnT", [P, SEQ])
        wqk_f = probs1[:].rearrange("p i g s -> p i (g s)")
        c_rows = oT[:].rearrange("p g s -> p (g s)").rearrange("p (b n) -> p b n", n=P)
        gsign = probs0[:, 0, :, :].rearrange("p g s -> p (g s)").rearrange("p (b d) -> p b d", d=D)
        gabs = probs0[:, 1, :, :].rearrange("p g s -> p (g s)").rearrange("p (b d) -> p b d", d=D)
        lmax = sb("lmax", [P, TILES])
        lshift = sb("lshift", [P, TILES, OPEN])
        prob = sb("prob", [P, TILES, OPEN])
        above = sb("above", [P, TILES, OPEN, OPEN])
        same = sb("same", [P, TILES, OPEN, OPEN])
        rank = sb("rank", [P, TILES, OPEN])
        kept = sb("kept", [P, TILES, OPEN])
        ksum = sb("ksum", [P, TILES])
        krec = sb("krec", [P, TILES])
        share = sb("share", [P, TILES, OPEN])
        share_cut = sb("share_cut", [P, TILES, 2 * OPEN], fp32r)
        x1 = x_sb
        h2 = sb("h2", [P, SEQ])
        h2T = sb("h2T", [P, NBATCH * SEQ])
        h2_hi = sb("h2_hi", [P, NBATCH * SEQ], fp32r)
        h2_lo = sb("h2_lo", [P, NBATCH * SEQ], fp32r)
        shareT = sb("shareT", [2 * OPEN, NBATCH * SEQ], fp32r)
        xw_hi = sb("xw_hi", [P, 2, SEQ], fp32r)
        xw_lo = sb("xw_lo", [P, 2, SEQ], fp32r)
        hid_hi = sb("hid_hi", [P, SLOTS, SEQ], fp32r)
        hid_lo = sb("hid_lo", [P, SLOTS, SEQ], fp32r)
        work = sb("work", [P, SLOTS + 8, SEQ])
        hid, th, glu = work[:, 0:SLOTS, :], work[:, SLOTS:SLOTS + 2, :], work[:, SLOTS + 2:SLOTS + 4, :]
        xw, pair_share, yT = (work[:, SLOTS + n, :] for n in (4, 5, 6))
        y_out = work[:, SLOTS + 7, :].rearrange("p (t d) -> p t d", t=TILES)
        w_raw = work[:].rearrange("p n c -> p (n c)")[:, 0:UNITS * P].rearrange("p (u f) -> p u f", f=P)
        wmod_sb = h2T[:, 0:NMOD * D]
        spare = h2T[:, NMOD * D:NBATCH * SEQ].rearrange("p (n d) -> p n d", d=D)
        sel_f = spare[0:2 * OPEN, 0:OPEN + PAIRS, :]
        c_exp, c_rec, c_silu = (spare[0:NBATCH, OPEN + PAIRS + n, :] for n in range(3))

        A = [ctx.enter_context(nc.psum_tensor(f"A{i}", [P, 2 * BANK], fp32)) for i in range(2)]
        T = ctx.enter_context(nc.psum_tensor("T", [P, BANK], fp32))
        G = ctx.enter_context(nc.psum_tensor("G", [P, BANK], fp32))
        U = ctx.enter_context(nc.psum_tensor("U", [P, BANK], fp32))
        Y = ctx.enter_context(nc.psum_tensor("Y", [P, BANK], fp32))

        x0_in = sem("x0_in")
        x_in = sem("x_in")
        attn_w_in = sem("attn_w_in")
        mod_in = sem("mod_in")
        w1_in = sem("w1_in")
        w3_in = sem("w3_in")
        w2_in = sem("w2_in")
        pool_const = sem("pool_const")
        consts = sem("consts")
        wqk_step = sem("wqk_step")
        wqk_hi_ready = sem("wqk_hi_ready")
        wqk_ready = sem("wqk_ready")
        setup_dve = sem("setup_dve")
        setup_pe = sem("setup_pe")
        setup_act = sem("setup_act")
        w_cut_hi = sem("w_cut_hi")
        w_cut = sem("w_cut")
        a_written = sem("a_written")
        a_read = sem("a_read")
        t_written = sem("t_written")
        t_read = sem("t_read")
        var_ready = sem("var_ready")
        rstd_ready = sem("rstd_ready")
        xn_ready = sem("xn_ready")
        masked = sem("masked")
        hi_ready = sem("hi_ready")
        lo_ready = sem("lo_ready")
        cut_ready = sem("cut_ready")
        prob_ready = sem("prob_ready")
        share_ready = sem("share_ready")
        dve_step = sem("dve_step")
        h2_hi_ready = sem("h2_hi_ready")
        h2_cut = sem("h2_cut")
        h2_kept = sem("h2_kept")
        xw_hi_ready = sem("xw_hi_ready")
        xw_cut = sem("xw_cut")
        g_written = sem("g_written")
        g_read = sem("g_read")
        u_written = sem("u_written")
        u_read = sem("u_read")
        tanh_done = sem("tanh_done")
        scaled = sem("scaled")
        hid_hi_ready = sem("hid_hi_ready")
        hid_cut = sem("hid_cut")
        down_done = sem("down_done")
        y_read = sem("y_read")
        out_sent = sem("out_sent")
        out_free = sem("out_free")
        waits_apart = sem("waits_apart")

        SETUP = 1
        N_A, N_T = 3 + 4 * GROUPS, 8 + GROUPS
        A_Q, A_K, A_S, A_E, A_O = 0, 1, 2, 2 + 2 * GROUPS, 2 + 4 * GROUPS
        (T_XN, T_V, T_MAX), T_PV = range(3), 3
        T_ATTN, T_WO, T_H2, T_LOGIT, T_SHARE = range(3 + GROUPS, 8 + GROUPS)
        G_USES = ([("share", 0), ("share", 1), ("share", OPEN)] + [("block", u) for u in range(FULL + 1)]
                  + [("share", 2)] + [("block", u) for u in range(FULL + 1, FULL + 4)] + [("share", OPEN + 1)]
                  + [("block", u) for u in range(FULL + 4, UP + 1)] + [("share", 3)]
                  + [("block", u) for u in range(UP + 1, UNITS)] + [("output", 0)])
        N_G = len(G_USES)
        assert PAIRS == 2 and FULL + 4 <= UP

        def attention_steps(cuts=()):
            S, E, W = "scores", "exps", "weigh"
            lots = [[("norm1",)], [("xnT",)], [("proj",)], [("v",), (S, 0, 0)]]
            lots += [[(S, n // 2, n % 2)] for n in range(1, 2 * GROUPS)]
            lots += [[("peaks",)], [(E, 0)], [(E, 1), (W, 0)], [(E, 2), (W, 1)], [(E, 3), (W, 2)], [(W, 3)],
                     [("back",)], [("attnT",)], [("wo",)], [("norm2",)], [("h2T",)], [("logits",)],
                     [("share",)]]
            return lots

        ATTENTION, EXPERTS = "attention", "experts"
        A_LOTS = attention_steps()

        def merged():
            after = {0: 3, 1: 1, 2: 3, 3: 1, 4: 1, 5: 1, 6: 1, 7: 1, 8: 1, 9: 1, 10: 1, 11: 1, 12: 1,
                     13: 1, 14: 1, 15: 1, 16: 2, 17: 1, 18: 1, 19: 2, 20: 1, 21: 1, 22: 1}
            uses, order = list(G_USES), []
            for n, lot in enumerate(A_LOTS):
                order += [(ATTENTION, step) for step in lot]
                order += [(EXPERTS, uses.pop(0)) for _ in range(min(after.get(n, 0), len(uses)))]
            assert not uses, uses
            return order

        MERGED = merged()
        FIRST = [(ATTENTION, step) for lot in A_LOTS for step in lot]
        for weight, behind in (("w2", ("back",)), ("w3", ("scores", 2, 0)), ("w1", ("proj",))):
            FIRST.insert(FIRST.index((ATTENTION, behind)) + 1, ("cut", weight))
        LAST = [(EXPERTS, use) for use in G_USES]

        def run(eng, attention, experts, cut_weight=None):
            for part, step in FIRST:
                if part == ATTENTION:
                    attention(0, *step)
                elif cut_weight:
                    cut_weight(step)
            with eng.Fori(0, NBATCH - 1) as b:
                for part, step in MERGED:
                    if part == ATTENTION:
                        attention(b + 1, *step)
                    else:
                        experts(b, *step)
            for part, step in LAST:
                experts(NBATCH - 1, *step)

        block = ctx.enter_context(nc.Block())

        def two_heads(n):
            return A[n % 2][:].rearrange("p (h i t) -> p h i t", h=2, i=TILES)

        def wait_apart(eng, s, value):
            eng.wait_ge(s, value)
            eng.sem_inc(waits_apart, 1)

        def unit_rows(w, raw, eng, s):
            n = 0
            for pair in range(PAIRS):
                e, u = 2 * pair, pair * UP
                flat = raw[:, u:u + UP, :].rearrange("p u f -> p (u f)")
                eng.dma_start(flat[:, 0:HID], w[e, :, :]).then_inc(s, 16)
                eng.dma_start(flat[:, HID:HID + HALF], w[e + 1, :, FULL * P:HID]).then_inc(s, 16)
                eng.dma_start(flat[:, HID + HALF:2 * HID], w[e + 1, :, 0:FULL * P]).then_inc(s, 16)
                n += 48
            return n
        W_IN = 48 * PAIRS

        @block.sync
        def _(sp):
            sp.dma_start(x_sb[:, 0:TILES, :],
                         h[0, :, :].rearrange("(t p) d -> p t d", p=P)).then_inc(x0_in, 16)
            sp.dma_start(wqvk_sb[:], wqvk).then_inc(attn_w_in, 16)
            sp.dma_start(wo_sb[:], wo).then_inc(attn_w_in, 16)
            sp.dma_start(x_sb[:, TILES:, :], h[1:, :, :].rearrange("b (t p) d -> p (b t) d", p=P)
                         ).then_inc(x_in, 16)
            unit_rows(w1, w_raw, sp, w1_in)
            sp.wait_ge(w_cut, 1)
            unit_rows(w3, w_raw, sp, w3_in)
            sp.wait_ge(w_cut, 2)
            for pair in range(PAIRS):
                e, u = 2 * pair, pair * UP
                sp.dma_start(w_raw[:, u:u + FULL, :],
                             w2[e, 0:FULL * P, :].rearrange("(u p) d -> p u d", p=P)).then_inc(w2_in, 16)
                sp.dma_start(w_raw[0:HALF, u + FULL, :], w2[e, FULL * P:HID, :]).then_inc(w2_in, 16)
                sp.dma_start(w_raw[HALF:P, u + FULL, :], w2[e + 1, FULL * P:HID, :]).then_inc(w2_in, 16)
                sp.dma_start(w_raw[:, u + FULL + 1:u + UP, :],
                             w2[e + 1, 0:FULL * P, :].rearrange("(u p) d -> p u d", p=P)).then_inc(w2_in, 16)
            sp.sem_inc(out_free, 1)
            with sp.Fori(0, NBATCH) as b:
                sp.wait_ge(g_read, SETUP + b * N_G + N_G)
                sp.dma_start(out[bass.ds(b, 1), :, :].rearrange("b (t p) d -> p (b t) d", p=P),
                             y_out).then_inc(out_sent, 16)
                sp.wait_ge(out_sent, 16 * b + 16)
                sp.sem_inc(out_free, 1)

        CUTS = {"w1": (w1_in, W_IN, w1_hi, w1_lo, 1), "w3": (w3_in, W_IN, w3_hi, w3_lo, 2),
                "w2": (w2_in, 64 * PAIRS, w2_hi, w2_lo, 3)}

        @block.gpsimd
        def _(pool):
            nc.gpsimd.memset(ident[:], 0.0).then_inc(pool_const, 1)
            nc.gpsimd.memset(causal_bf[:], 0.0).then_inc(pool_const, 1)
            nc.gpsimd.memset(sel_f, 0.0).then_inc(pool_const, 1)
            nc.gpsimd.memset(before[:], 1.0).then_inc(pool_const, 1)
            nc.gpsimd.memset(minus_half[:], -0.5).then_inc(consts, 1)
            pool.wait_ge(pool_const, 4)
            nc.gpsimd.affine_select(out=ident[:], in_=ident[:], compare_op=ALU.not_equal, fill=1.0, base=0,
                                    pattern=[[-1, P]], channel_multiplier=1).then_inc(consts, 1)
            nc.gpsimd.affine_select(out=causal_bf[:], in_=causal_bf[:], compare_op=ALU.is_ge, fill=MASKED,
                                    base=0, pattern=[[0, 2], [-1, P]], channel_multiplier=1).then_inc(consts, 1)
            nc.gpsimd.affine_select(out=before[:], in_=before[:], compare_op=ALU.is_ge, fill=0.0, base=-1,
                                    pattern=[[1, OPEN], [-1, OPEN]], channel_multiplier=0).then_inc(consts, 1)
            for n, base in enumerate((0, -OPEN)):
                if n:
                    pool.wait_ge(pool_const, 6)
                nc.gpsimd.affine_select(out=sel_f[:, 0:OPEN, :], in_=sel_f[:, 0:OPEN, :],
                                        compare_op=ALU.not_equal, fill=1.0, base=base,
                                        pattern=[[-1, OPEN], [0, P]], channel_multiplier=1
                                        ).then_inc(pool_const, 1)
                halves = sel_f[:, OPEN:, :].rearrange("p m (s f) -> p m s f", s=2)
                nc.gpsimd.affine_select(out=halves, in_=halves, compare_op=ALU.not_equal, fill=1.0,
                                        base=base, pattern=[[-2, PAIRS], [-1, 2], [0, HALF]],
                                        channel_multiplier=1).then_inc(pool_const, 1)
            pool.wait_ge(wqk_hi_ready, 1)
            nc.gpsimd.tensor_tensor(wqk_lo[:], wqk_f, wqk_hi[:].bitcast(fp32),
                                    ALU.subtract).then_inc(wqk_ready, 1)

            def left(out, value, hi):
                return nc.gpsimd.tensor_tensor(out, value, hi.bitcast(fp32), ALU.subtract)

            def attention(b, part, *at):
                if part in ("norm1", "norm2"):
                    k = int(part == "norm2")
                    pool.wait_ge(var_ready, b * 2 + k + 1)
                    nc.gpsimd.tensor_tensor(rstd[:, k, :], veps[:, k, :], minus_half[:],
                                            ALU.pow).then_inc(rstd_ready, 1)
                elif part == "xnT":
                    pool.wait_ge(hi_ready, b + 1)
                    left(hT_lo[:], hT[:], hT_hi[:]).then_inc(lo_ready, 1)
                elif part == "exps":
                    g, = at
                    wait_apart(pool, a_read, SETUP + b * N_A + A_E + 2 * g + 2)
                    for pr in (probs0, probs1):
                        band = pr[:, g % 2, :, 0:P]
                        nc.gpsimd.affine_select(out=band, in_=band, compare_op=ALU.is_ge, fill=0.0, base=0,
                                                pattern=[[0, GROUP], [1, P]], channel_multiplier=-1
                                                ).then_inc(masked, 1)
                elif part == "h2T":
                    pool.wait_ge(h2_hi_ready, b + 1)
                    left(h2_lo[:, bass.ds(b * SEQ, SEQ)], h2[:],
                         h2_hi[:, bass.ds(b * SEQ, SEQ)]).then_inc(h2_cut, 1)

            def experts(b, part, n):
                if part == "share" and n < OPEN:
                    pool.wait_ge(xw_hi_ready, b * OPEN + n + 1)
                    left(xw_lo[:, n % 2, :], xw, xw_hi[:, n % 2, :]).then_inc(xw_cut, 1)
                elif part == "output" or part == "block" and n:
                    n = n - 1 if part == "block" else UNITS - 1
                    slot = n % SLOTS
                    pool.wait_ge(hid_hi_ready, b * UNITS + n + 1)
                    left(hid_lo[:, slot, :], hid[:, slot, :], hid_hi[:, slot, :]).then_inc(hid_cut, 1)

            def cut_weight(name):
                _, _, hi, lo, n = CUTS[name]
                pool.wait_ge(w_cut_hi, n)
                left(lo[:], w_raw, hi[:]).then_inc(w_cut, 1)

            run(pool, attention, experts, cut_weight)

        @block.scalar
        def _(act):
            act.dma_start(c_sb[:], c).then_inc(mod_in, 16)
            act.dma_start(gate_sb[:], gate_w[0:OPEN, :]).then_inc(mod_in, 16)
            act.dma_start(wmod_sb, wmod).then_inc(mod_in, 16)
            act.wait_ge(mod_in, 48)
            nc.scalar.activation(c_exp, c_sb[:], ACT.Exp, scale=-1.0).then_inc(setup_act, 1)
            act.wait_ge(wqk_step, 4)
            nc.scalar.activation(wqk_hi[:], wqk_f, ACT.Copy).then_inc(wqk_hi_ready, 1)

            def attention(b, part, *at):
                if part == "xnT":
                    act.wait_ge(t_read, SETUP + b * N_T + T_XN + 1)
                    nc.scalar.activation(hT_hi[:], hT[:], ACT.Copy).then_inc(hi_ready, 1)
                elif part == "proj":
                    act.wait_ge(a_written, b * N_A + A_Q + 1)
                    nc.scalar.activation(cut[:, 0, :, :], A[0][:].rearrange("p (g s) -> p g s", g=GROUPS),
                                         ACT.Copy).then_inc(cut_ready, 1)
                    act.wait_ge(a_written, b * N_A + A_K + 1)
                    for g in range(GROUPS):
                        last = nc.scalar.activation(cut[:, 1, g, :], A[1][:, g * SEQ:(g + 1) * SEQ],
                                                    ACT.Identity, bias=minus_row[:, g:g + 1])
                    last.then_inc(cut_ready, 1)
                elif part == "v":
                    act.wait_ge(t_written, b * N_T + T_V + 1)
                    nc.scalar.activation(v_ones[:, :, :, 0:HD].rearrange("p t h d -> p (t h) d"),
                                         T[:, 0:SEQ].rearrange("p (n d) -> p n d", d=HD),
                                         ACT.Copy).then_inc(t_read, 1)
                elif part == "exps":
                    g, = at
                    for hp in range(2):
                        n = A_E + 2 * g + hp
                        act.wait_ge(a_written, b * N_A + n + 1)
                        if g >= 2 and hp == 0:
                            act.wait_ge(t_written, b * N_T + T_PV + g - 1)
                        s, heads = two_heads(n), slice(2 * hp, 2 * hp + 2)
                        nc.scalar.activation(probs0[:, g % 2, heads, :], s[:, :, 0, :], ACT.Exp,
                                             scale=SCORE_SCALE)
                        nc.scalar.activation(probs1[:, g % 2, heads, :], s[:, :, 1, P:SEQ], ACT.Exp,
                                             scale=SCORE_SCALE).then_inc(a_read, 1)
                elif part == "weigh":
                    g, = at
                    act.wait_ge(t_written, b * N_T + T_PV + g + 1)
                    nc.scalar.activation(oT[:, g, :], T[:, 0:SEQ], ACT.Copy).then_inc(t_read, 1)
                elif part == "attnT":
                    act.wait_ge(t_written, b * N_T + T_ATTN + 1)
                    nc.scalar.activation(attnT[:], T[:, 0:SEQ], ACT.Copy).then_inc(t_read, 1)
                elif part == "h2T":
                    act.wait_ge(t_read, SETUP + b * N_T + T_H2 + 1)
                    nc.scalar.activation(h2_hi[:, bass.ds(b * SEQ, SEQ)], h2[:],
                                         ACT.Copy).then_inc(h2_hi_ready, 1)
                    nc.scalar.activation(h2T[:, bass.ds(b * SEQ, SEQ)], h2[:], ACT.Copy).then_inc(h2_kept, 1)
                elif part == "logits":
                    act.wait_ge(t_read, SETUP + b * N_T + T_LOGIT + 1)
                    nc.scalar.activation(prob[:], lshift[:], ACT.Exp).then_inc(prob_ready, 1)

            def experts(b, part, n):
                use = b * N_G + G_USES.index((part, n)) + 1
                if part == "share" and n < OPEN:
                    act.wait_ge(g_read, SETUP + use)
                    if n >= 2:
                        act.wait_ge(u_written, SETUP + b * UNITS + (FULL if n == 2 else UP))
                    nc.scalar.activation(xw_hi[:, n % 2, :], xw, ACT.Copy).then_inc(xw_hi_ready, 1)
                elif part == "share":
                    act.wait_ge(g_written, use)
                    nc.scalar.activation(pair_share, G[:, 0:SEQ], ACT.Copy).then_inc(g_read, 1)
                elif part == "block":
                    act.wait_ge(g_written, use)
                    nc.scalar.activation(th[:, n % 2, :], G[:, 0:SEQ], ACT.Tanh, scale=0.5).then_inc(tanh_done, 1)
                    round_hidden(b, n - 1)
                elif part == "output":
                    round_hidden(b, UNITS - 1)

            def round_hidden(b, n):
                if n < 0:
                    return
                act.wait_ge(u_read, SETUP + b * UNITS + n + 1)
                if n % UP == FULL:
                    act.wait_ge(scaled, b * PAIRS + n // UP + 1)
                if n >= SLOTS:
                    act.wait_ge(down_done, b * UNITS + n - SLOTS + 1)
                nc.scalar.activation(hid_hi[:, n % SLOTS, :], hid[:, n % SLOTS, :],
                                     ACT.Copy).then_inc(hid_hi_ready, 1)

            def cut_weight(name):
                s, full, hi, _, _ = CUTS[name]
                act.wait_ge(s, full)
                nc.scalar.activation(hi[:], w_raw, ACT.Copy).then_inc(w_cut_hi, 1)

            run(act, attention, experts, cut_weight)

        @block.tensor
        def _(pe):
            def cut_product(dst, w_hi, w_lo, x_hi, x_lo, start=True, stop=True):
                nc.tensor.matmul(dst, w_hi, x_hi, start=start, stop=False)
                nc.tensor.matmul(dst, w_hi, x_lo, start=False, stop=False)
                return nc.tensor.matmul(dst, w_lo, x_hi, start=False, stop=stop)

            pe.wait_ge(consts, 4)
            pe.wait_ge(mod_in, 48)
            nc.tensor.transpose(T[:, 0:OPEN], gate_sb[:], ident[0:OPEN, 0:OPEN]).then_inc(setup_pe, 1)
            pe.wait_ge(setup_dve, 3)
            nc.tensor.transpose(G[:, 0:NBATCH], c_silu, ident[0:NBATCH, 0:NBATCH]).then_inc(setup_pe, 1)
            pe.wait_ge(setup_dve, 4)
            for m in range(NMOD):
                last = nc.tensor.matmul(U[:, m * NBATCH:(m + 1) * NBATCH], wmod_sb[:, m * D:(m + 1) * D],
                                        cT[:], start=True, stop=True)
            last.then_inc(u_written, 1)
            for b in range(NBATCH):
                last = nc.tensor.matmul(A[0][:, b * D:(b + 1) * D], c_rows[:, b, :], wmod_sb[:, 2 * D:3 * D],
                                        start=True, stop=True)
            last.then_inc(setup_pe, 1)
            pe.wait_ge(attn_w_in, 32)

            def attention(b, part, *at):
                def t_free(n):
                    pe.wait_ge(t_read, SETUP + b * N_T + n)

                def a_free(n):
                    pe.wait_ge(a_read, SETUP + b * N_A + max(n - 1, 0))

                def transposed(src, t):
                    for i in range(TILES):
                        last = nc.tensor.transpose(T[:, i * P:(i + 1) * P], src(i), ident[:])
                    last.then_inc(t_written, 1)

                if part == "xnT":
                    pe.wait_ge(xn_ready, b * 2 + 1)
                    t_free(T_XN)
                    transposed(lambda i: xn[:, 0, i, :], T_XN)
                elif part == "proj":
                    pe.wait_ge(lo_ready, b + 1)
                    pe.wait_ge(wqk_ready, 1)
                    for n in (A_Q, A_K):
                        a_free(n)
                        for g in range(GROUPS):
                            cols = slice(g * P, (g + 1) * P)
                            last = cut_product(A[n][:, g * SEQ:(g + 1) * SEQ], wqk_hi[:, n, cols],
                                               wqk_lo[:, n, cols], hT_hi[:], hT_lo[:])
                        last.then_inc(a_written, 1)
                elif part == "v":
                    t_free(T_V)
                    for i in range(TILES):
                        last = nc.tensor.matmul(T[:, i * P:(i + 1) * P], hT[:, i * P:(i + 1) * P],
                                                wqvk_sb[:, D:2 * D], start=True, stop=True)
                    last.then_inc(t_written, 1)
                elif part == "scores":
                    g, hp = at
                    n = A_S + 2 * g + hp
                    a_free(n)
                    if n == A_S:
                        pe.wait_ge(a_read, SETUP + b * N_A + 2)
                    dst = two_heads(n)
                    for k in range(2):
                        blocks = dst[:, k, :, :].rearrange("p i t -> p (i t)").rearrange(
                            "p (n t) -> p n t", t=P)
                        nc.tensor.matmul(blocks[:, 0:4:3, :], ident_bf[:], causal_bf[:], start=True, stop=True)
                    for i in range(TILES):
                        for k in range(2):
                            rows = slice((2 * hp + k) * STRIP, (2 * hp + k + 1) * STRIP)
                            last = nc.tensor.matmul(dst[:, k, i, :], q_rows[rows, g, i * P:(i + 1) * P],
                                                    k_rows[rows, g, :], start=False, stop=True,
                                                    skip_group_check=True)
                    last.then_inc(a_written, 1)
                elif part == "peaks":
                    pe.wait_ge(a_read, SETUP + b * N_A + A_E)
                    t_free(T_MAX)
                    transposed(lambda i: peak[:, i, :, :].rearrange("p j r -> p (j r)"), T_MAX)
                elif part == "exps":
                    g, = at
                    if g == 0:
                        t_free(T_MAX + 1)
                    for hp in range(2):
                        n = A_E + 2 * g + hp
                        a_free(n)
                        dst = two_heads(n)
                        for i in range(TILES):
                            for k in range(2):
                                rows = slice((2 * hp + k) * STRIP, (2 * hp + k + 1) * STRIP)
                                last = nc.tensor.matmul(dst[:, k, i, :], k_rows[rows, g, i * P:(i + 1) * P],
                                                        q_max[rows, g, :], start=i == 0, stop=True,
                                                        skip_group_check=True)
                        last.then_inc(a_written, 1)
                elif part == "weigh":
                    g, = at
                    t_free(T_PV + g)
                    pe.wait_ge(masked, b * 2 * GROUPS + 2 * g + 2)
                    for j in range(GROUP):
                        nc.tensor.matmul(T[j * STRIP:(j + 1) * STRIP, 0:SEQ], v_ones[:, 0, g * GROUP + j, :],
                                         probs0[:, g % 2, j, :], start=True, stop=False)
                    for j in range(GROUP):
                        last = nc.tensor.matmul(T[j * STRIP:(j + 1) * STRIP, P:SEQ],
                                                v_ones[:, 1, g * GROUP + j, :], probs1[:, g % 2, j, :],
                                                start=False, stop=True)
                    last.then_inc(t_written, 1)
                elif part == "back":
                    a_free(A_O)
                    t_free(T_ATTN)
                    for i in range(TILES):
                        for g in range(GROUPS):
                            last = nc.tensor.transpose(A[0][:, i * BANK + g * P:i * BANK + (g + 1) * P],
                                                       oT[:, g, i * P:(i + 1) * P], ident[:])
                    last.then_inc(a_written, 1)
                elif part == "attnT":
                    pe.wait_ge(a_read, SETUP + b * N_A + N_A)
                    transposed(lambda i: attn[:, i, :, :].rearrange("p h d -> p (h d)"), T_ATTN)
                elif part == "wo":
                    t_free(T_WO)
                    for i in range(TILES):
                        last = nc.tensor.matmul(T[:, i * D:(i + 1) * D], attnT[:, i * P:(i + 1) * P],
                                                wo_gated[:, bass.ds(b, 1), :].rearrange("p a d -> p (a d)"),
                                                start=True, stop=True)
                    last.then_inc(t_written, 1)
                elif part == "h2T":
                    pe.wait_ge(xn_ready, b * 2 + 2)
                    transposed(lambda i: xn[:, 1, i, :], T_H2)
                elif part == "logits":
                    t_free(T_LOGIT)
                    for i in range(TILES):
                        last = nc.tensor.matmul(T[:, i * OPEN:(i + 1) * OPEN], h2[:, i * P:(i + 1) * P],
                                                gate_wT[:], start=True, stop=True)
                    last.then_inc(t_written, 1)
                elif part == "share":
                    pe.wait_ge(share_ready, b + 1)
                    for i in range(TILES):
                        last = nc.tensor.transpose(T[0:2 * OPEN, i * P:(i + 1) * P],
                                                   share_cut[:, i, :].bitcast(fp32), ident[:])
                    last.then_inc(t_written, 1)

            def down(b, u):
                pe.wait_ge(hid_cut, b * UNITS + u + 1)
                cut_product(Y[:, 0:SEQ], w2_hi[:, u, :], w2_lo[:, u, :], hid_hi[:, u % SLOTS, :],
                            hid_lo[:, u % SLOTS, :], start=u == 0, stop=u == UNITS - 1).then_inc(down_done, 1)

            def experts(b, part, n):
                tokens = bass.ds(b * SEQ, SEQ)
                use = b * N_G + G_USES.index((part, n))
                if part == "share":
                    if n == 0:
                        pe.wait_ge(t_read, SETUP + b * N_T + N_T)
                    wait_apart(pe, g_read, SETUP + use)
                    nc.tensor.matmul(G[:, 0:SEQ], sel[:, n, :], shareT[:, tokens], start=True,
                                     stop=True).then_inc(g_written, 1)
                elif part == "block":
                    if n == 0:
                        pe.wait_ge(h2_cut, b + 1)
                        pe.wait_ge(w_cut, 3)
                    pe.wait_ge(g_read, SETUP + use)
                    cut_product(G[:, 0:SEQ], w1_hi[:, n, :], w1_lo[:, n, :], h2_hi[:, tokens],
                                h2_lo[:, tokens]).then_inc(g_written, 1)
                    s = expert_of(n % UP)
                    if n % UP in (0, FULL + 1):
                        pe.wait_ge(xw_cut, b * OPEN + 2 * (n // UP) + s + 1)
                    pe.wait_ge(u_read, SETUP + b * UNITS + n)
                    xs = (h2_hi[:, tokens], h2_lo[:, tokens]) if s is None else \
                        (xw_hi[:, s, :], xw_lo[:, s, :])
                    cut_product(U[:, 0:SEQ], w3_hi[:, n, :], w3_lo[:, n, :], *xs).then_inc(u_written, 1)
                    if n >= LAG:
                        down(b, n - LAG)
                else:
                    for u in range(UNITS - LAG, UNITS):
                        down(b, u)
                    pe.wait_ge(g_read, SETUP + use)
                    pe.wait_ge(y_read, b + 1)
                    for i in range(TILES):
                        last = nc.tensor.transpose(G[:, i * P:(i + 1) * P], yT[:, i * P:(i + 1) * P], ident[:])
                    last.then_inc(g_written, 1)

            run(pe, attention, experts)

        @block.vector
        def _(dve):
            done = [0]

            def setup(ins):
                done[0] += 1
                ins.then_inc(setup_dve, 1)
                dve.wait_ge(setup_dve, done[0])

            dve.wait_ge(setup_act, 1)
            setup(nc.vector.tensor_scalar_add(c_exp, c_exp, 1.0))
            setup(nc.vector.reciprocal(c_rec, c_exp))
            setup(nc.vector.tensor_tensor(c_silu, c_sb[:], c_rec, ALU.mult))
            dve.wait_ge(setup_pe, 1)
            nc.vector.tensor_copy(gate_wT[:], T[:, 0:OPEN]).then_inc(t_read, 1)
            dve.wait_ge(setup_pe, 2)
            nc.vector.tensor_copy(cT[:], G[:, 0:NBATCH]).then_inc(g_read, 1)
            dve.wait_ge(g_read, SETUP)
            setup(nc.vector.tensor_copy(c_rows, cT[:].unsqueeze(2).to_broadcast([P, NBATCH, P])))
            dve.wait_ge(u_written, SETUP)
            m_ps = U[:, 0:NMOD * NBATCH].rearrange("p (m b) -> p m b", m=NMOD)
            nc.vector.tensor_copy(mod[:, 0, :], m_ps[:, 0, :]).then_inc(u_read, 1)
            nc.vector.tensor_scalar_add(mod[:, 1, :], m_ps[:, 1, :], 1.0)
            nc.vector.tensor_copy(mod[:, 3, :], m_ps[:, 3, :])
            nc.vector.tensor_scalar_add(mod[:, 4, :], m_ps[:, 4, :], 1.0)
            def clamp(dst, g, sign, size):
                nc.vector.tensor_copy(size, g)
                setup(nc.vector.tensor_scalar(sign, g, 0.0, 2.0, ALU.is_ge, ALU.mult))
                setup(nc.vector.tensor_scalar_add(sign, sign, -1.0))
                setup(nc.vector.scalar_tensor_tensor(out=size, in0=size, scalar=-1.0, in1=size,
                                                     op0=ALU.mult, op1=ALU.max))
                setup(nc.vector.scalar_tensor_tensor(out=dst, in0=size, scalar=GATE_FLOOR, in1=sign,
                                                     op0=ALU.max, op1=ALU.mult))

            flat_sign, flat_size = (t.rearrange("p b d -> p (b d)") for t in (gsign, gabs))
            clamp(mod[:, 5, :], m_ps[:, 5, :], flat_sign[:, 0:NBATCH], flat_size[:, 0:NBATCH])
            dve.wait_ge(setup_pe, 3)
            dve.wait_ge(attn_w_in, 32)
            clamp(flat_size, A[0][:], flat_sign, flat_size)
            nc.vector.tensor_tensor(wo_gated[:], gabs, wo_sb[:].unsqueeze(1).to_broadcast([P, NBATCH, D]),
                                    ALU.mult).then_inc(a_read, 1)
            dve.wait_ge(consts, 4)
            nc.vector.tensor_copy(ident_bf[:], ident[:])
            nc.vector.memset(v_ones[:], 0.0).then_inc(wqk_step, 1)
            nc.vector.memset(peak[:], 0.0).then_inc(wqk_step, 1)
            nc.vector.memset(wqk_f, 0.0).then_inc(wqk_step, 1)
            dve.wait_ge(wqk_step, 3)
            for n, at in ((0, 0), (1, 2 * D)):
                dst = wqk_f[:, n, :].rearrange("p (h r) -> p h r", r=STRIP)
                for r in range(REP):
                    last = nc.vector.tensor_copy(dst[:, :, r * HD:(r + 1) * HD],
                                                 wqvk_sb[:, at:at + D].rearrange("p (h d) -> p h d", d=HD))
            last.then_inc(wqk_step, 1)
            nc.vector.memset(v_ones[:, :, :, HD:HD + 1], 1.0)
            id_rows = ident[:].rearrange("p (j r) -> p j r", r=STRIP)
            nc.vector.tensor_reduce(low_q[:], id_rows[:, :, 2 * HD:3 * HD], AX.XY, ALU.add, negate=True)
            nc.vector.tensor_reduce(row_tmp[:, 0:1], id_rows[:, :, HD:2 * HD], AX.XY, ALU.add)
            nc.vector.tensor_reduce(row_tmp[:, 1:2], id_rows[:, :, REP * HD:REP * HD + GROUPS], AX.XY, ALU.add)
            nc.vector.tensor_reduce(minus_row[:], id_rows[:, :, REP * HD:REP * HD + GROUPS].rearrange(
                "p j g -> p g j"), AX.X, ALU.add, negate=True)
            dve.wait_ge(pool_const, 8)
            nc.vector.tensor_copy(sel[:], sel_f).then_inc(wqk_step, 1)
            dve.wait_ge(wqk_step, 5)
            nc.vector.tensor_tensor(low_k[:], row_tmp[:, 1:2], row_tmp[:, 0:1],
                                    ALU.subtract).then_inc(wqk_step, 1)
            dve.wait_ge(wqk_step, 6)

            STEPS = 15
            step = [0]

            def attention(b, part, *at):
                if part == "norm1":
                    step[0] = 0

                def then(ins):
                    step[0] += 1
                    ins.then_inc(dve_step, 1)
                    wait_apart(dve, dve_step, b * STEPS + step[0])

                def t_wait(n):
                    dve.wait_ge(t_written, b * N_T + n + 1)

                def norm(src, k):
                    for i in range(TILES):
                        ins = nc.vector.bn_stats(stats[:, k, i, :], src[:, bass.ds(b * TILES + i, 1), :]
                                                 .rearrange("p a d -> p (a d)"))
                    then(ins)
                    for i in range(TILES):
                        ins = nc.vector.bn_aggr(mv[:, k, i, :], stats[:, k, i, :])
                    then(ins)
                    nc.vector.tensor_scalar_add(veps[:, k, :], mv[:, k, :, 1], LN_EPS).then_inc(var_ready, 1)
                    dve.wait_ge(rstd_ready, b * 2 + k + 1)
                    for i in range(TILES):
                        ins = nc.vector.tensor_scalar(
                            xn[:, k, i, :], src[:, bass.ds(b * TILES + i, 1), :].rearrange("p a d -> p (a d)"),
                            mv[:, k, i, 0:1], rstd[:, k, i:i + 1], ALU.subtract, ALU.mult)
                    ins.then_inc(xn_ready, 1)

                if part == "norm1":
                    norm(x_sb, 0)
                elif part == "xnT":
                    t_wait(T_XN)
                    nc.vector.tensor_scalar(hT[:], T[:, 0:SEQ], mod[:, 1, bass.ds(b, 1)],
                                            mod[:, 0, bass.ds(b, 1)], ALU.mult, ALU.add).then_inc(t_read, 1)
                elif part == "proj":
                    for n, rows, low in ((A_Q, q_rows, low_q), (A_K, k_rows, low_k)):
                        dve.wait_ge(cut_ready, b * 2 + n + 1)
                        nc.vector.scalar_tensor_tensor(
                            out=rows[:].rearrange("p g s -> p (g s)"),
                            in0=cut[:, n, :, :].rearrange("p g s -> p (g s)").bitcast(fp32),
                            scalar=low[:, 0:1], in1=A[n][:], op0=ALU.mult, op1=ALU.add).then_inc(a_read, 1)
                elif part == "scores":
                    g, hp = at
                    n = A_S + 2 * g + hp
                    dve.wait_ge(a_written, b * N_A + n + 1)
                    for i in range(TILES):
                        ins = nc.vector.reduce_max(peak[:, i, 2 * hp:2 * hp + 2, REP * HD + g],
                                                   two_heads(n)[:, :, i, 0:(i + 1) * P], AX.X)
                    ins.then_inc(a_read, 1)
                elif part == "peaks":
                    t_wait(T_MAX)
                    nc.vector.tensor_tensor(q_max[:], q_rows[:].bitcast(fp32),
                                            T[:, 0:SEQ].unsqueeze(1).to_broadcast([P, GROUPS, SEQ]),
                                            ALU.add).then_inc(t_read, 1)
                elif part == "back":
                    dve.wait_ge(a_written, b * N_A + A_O + 1)
                    sums = A[0][:].rearrange("p (t h r) -> p t h r", t=TILES, r=STRIP)
                    then(nc.vector.reciprocal(rden[:], sums[:, :, :, HD]))
                    nc.vector.tensor_tensor(attn[:], sums[:, :, :, 0:HD],
                                            rden[:].unsqueeze(3).to_broadcast([P, TILES, HEADS, HD]),
                                            ALU.mult).then_inc(a_read, 1)
                elif part == "wo":
                    t_wait(T_WO)
                    tiles = bass.ds(b * TILES, TILES)
                    nc.vector.tensor_tensor(x1[:, tiles, :], x_sb[:, tiles, :],
                                            T[:, 0:SEQ].rearrange("p (t d) -> p t d", t=TILES),
                                            ALU.add).then_inc(t_read, 1)
                elif part == "norm2":
                    wait_apart(dve, t_read, SETUP + b * N_T + T_WO + 1)
                    norm(x1, 1)
                elif part == "h2T":
                    t_wait(T_H2)
                    nc.vector.tensor_scalar(h2[:], T[:, 0:SEQ], mod[:, 4, bass.ds(b, 1)],
                                            mod[:, 3, bass.ds(b, 1)], ALU.mult, ALU.add).then_inc(t_read, 1)
                elif part == "logits":
                    t_wait(T_LOGIT)
                    logits = T[:, 0:TILES * OPEN].rearrange("p (t e) -> p t e", e=OPEN)
                    then(nc.vector.reduce_max(lmax[:], logits, AX.X))
                    nc.vector.tensor_tensor(lshift[:], logits,
                                            lmax[:].unsqueeze(2).to_broadcast([P, TILES, OPEN]),
                                            ALU.subtract).then_inc(t_read, 1)
                elif part == "share":
                    dve.wait_ge(prob_ready, b + 1)
                    square = [P, TILES, OPEN, OPEN]
                    other = prob[:].unsqueeze(2).to_broadcast(square)
                    own = prob[:].unsqueeze(3).to_broadcast(square)
                    nc.vector.tensor_tensor(above[:], other, own, ALU.is_gt)
                    then(nc.vector.tensor_tensor(same[:], other, own, ALU.is_equal))
                    then(nc.vector.tensor_tensor(same[:], same[:], before[:].unsqueeze(1).to_broadcast(square),
                                                 ALU.mult))
                    then(nc.vector.tensor_tensor(above[:], above[:], same[:], ALU.add))
                    then(nc.vector.reduce_sum(rank[:], above[:], AX.X))
                    then(nc.vector.scalar_tensor_tensor(out=kept[:], in0=rank[:], scalar=2.0, in1=prob[:],
                                                        op0=ALU.is_lt, op1=ALU.mult))
                    then(nc.vector.reduce_sum(ksum[:], kept[:], AX.X))
                    then(nc.vector.reciprocal(krec[:], ksum[:]))
                    then(nc.vector.scalar_tensor_tensor(out=share[:], in0=kept[:], scalar=0.5,
                                                        in1=krec[:].unsqueeze(2).to_broadcast([P, TILES, OPEN]),
                                                        op0=ALU.mult, op1=ALU.mult))
                    then(nc.vector.tensor_copy(share_cut[:, :, 0:OPEN], share[:]))
                    nc.vector.tensor_tensor(share_cut[:, :, OPEN:], share[:],
                                            share_cut[:, :, 0:OPEN].bitcast(fp32),
                                            ALU.subtract).then_inc(share_ready, 1)
                    t_wait(T_SHARE)
                    nc.vector.tensor_copy(shareT[:, bass.ds(b * SEQ, SEQ)],
                                          T[0:2 * OPEN, 0:SEQ]).then_inc(t_read, 1)
                    assert step[0] == STEPS, step[0]

            def experts(b, part, n):
                tokens = bass.ds(b * SEQ, SEQ)
                use = b * N_G + G_USES.index((part, n)) + 1
                if part == "share" and n < OPEN:
                    dve.wait_ge(g_written, use)
                    if n:
                        dve.wait_ge(xw_cut, b * OPEN + n)
                    else:
                        dve.wait_ge(h2_kept, b + 1)
                    nc.vector.tensor_tensor(xw, h2T[:, tokens], G[:, 0:SEQ], ALU.mult).then_inc(g_read, 1)
                elif part == "block":
                    dve.wait_ge(tanh_done, b * UNITS + n + 1)
                    nc.vector.scalar_tensor_tensor(out=glu[:, n % 2, :], in0=th[:, n % 2, :], scalar=1.0,
                                                   in1=G[:, 0:SEQ], op0=ALU.add, op1=ALU.mult
                                                   ).then_inc(g_read, 1)
                    dve.wait_ge(u_written, SETUP + b * UNITS + n + 1)
                    dve.wait_ge(g_read, SETUP + use)
                    if n >= SLOTS:
                        dve.wait_ge(hid_cut, b * UNITS + n - SLOTS + 1)
                    nc.vector.tensor_tensor(hid[:, n % SLOTS, :], glu[:, n % 2, :], U[:, 0:SEQ],
                                            ALU.mult).then_inc(u_read, 1)
                    if n % UP == FULL:
                        dve.wait_ge(u_read, SETUP + b * UNITS + n + 1)
                        dve.wait_ge(g_read, SETUP + b * N_G + G_USES.index(("share", OPEN + n // UP)) + 1)
                        nc.vector.tensor_tensor(hid[:, n % SLOTS, :], hid[:, n % SLOTS, :], pair_share,
                                                ALU.mult).then_inc(scaled, 1)
                elif part == "output":
                    dve.wait_ge(down_done, b * UNITS + UNITS)
                    nc.vector.tensor_scalar(yT, Y[:, 0:SEQ], mod[:, 5, bass.ds(b, 1)], None,
                                            ALU.mult).then_inc(y_read, 1)
                    dve.wait_ge(g_written, use)
                    dve.wait_ge(out_free, b + 1)
                    nc.vector.tensor_tensor(y_out, x1[:, bass.ds(b * TILES, TILES), :],
                                            G[:, 0:SEQ].rearrange("p (t d) -> p t d", t=TILES),
                                            ALU.add).then_inc(g_read, 1)

            dve.wait_ge(x0_in, 16)
            dve.wait_ge(x_in, 16)
            run(dve, attention, experts)


_INS = ['L0_attn_h', 'L0_attn_Wqvk', 'L0_attn_Wo', 'L0_ffn_gate_w', 'L0_ffn_w1', 'L0_ffn_w2', 'L0_ffn_w3',
        'L0_c', 'L0_wmod']


def kernel(**inputs):
    import numpy as _np
    import concourse.bacc as _bacc
    from concourse import mybir as _mybir
    from concourse.bass_utils import run_bass_kernel_spmd as _run

    nc = _bacc.Bacc("TRN2", target_bir_lowering=False, num_devices=1)
    arrays, args = {}, []
    for name in _INS:
        a = _np.ascontiguousarray(inputs[name])
        arrays[f"in_{name}_dram"] = a
        args.append(nc.dram_tensor(f"in_{name}_dram", a.shape, _mybir.dt.from_np(a.dtype), kind="ExternalInput").ap())
    shape = inputs['L0_attn_h'].shape
    args.append(nc.dram_tensor("out_0_dram", shape, _mybir.dt.float32, kind="ExternalOutput").ap())
    adaln_block_kernel(nc, *args)
    r = _run(nc, [arrays], core_ids=[0])
    return r.results[0]["out_0_dram"]
```

```python
import concourse.bass as bass
from concourse import mybir
from contextlib import ExitStack


def adaln_block_kernel(
    nc: bass.Bass,
    h: bass.AP,
    wqvk: bass.AP,
    wo: bass.AP,
    gate_w: bass.AP,
    w1: bass.AP,
    w2: bass.AP,
    w3: bass.AP,
    c: bass.AP,
    wmod: bass.AP,
    out: bass.AP,
):
    fp32, fp32r, bf16 = mybir.dt.float32, mybir.dt.float32r, mybir.dt.bfloat16
    ALU, ACT, AX = mybir.AluOpType, mybir.ActivationFunctionType, mybir.AxisListType

    NBATCH, SEQ, D = h.shape
    NMOD = wmod.shape[1] // D
    NEXP, _, HID = w1.shape
    OPEN = NEXP - 4
    HEADS = 16
    HD = D // HEADS
    SCORE_SCALE = float(D) ** -0.5
    LN_EPS = 1e-5
    GATE_FLOOR = 0.25
    MASKED = -1.0e30
    P = 128
    TILES = SEQ // P
    STRIP = 32
    GROUP = P // STRIP
    GROUPS = HEADS // GROUP
    REP = 3
    BANK = 512
    PAIRS = OPEN // 2
    FULL = HID // P
    HALF = HID - FULL * P
    assert 2 * HALF == P and SEQ == 2 * P
    UP = 2 * FULL + 1
    UNITS = PAIRS * UP
    LAG = 2
    TAIL_LAG = 3
    SLOTS = 4

    def expert_of(n):
        return 0 if n < FULL else None if n == FULL else 1

    ctx = ExitStack()
    with ctx:
        def sb(name, shape, dt=fp32):
            return ctx.enter_context(nc.sbuf_tensor(name, shape, dt))

        def sem(name):
            return ctx.enter_context(nc.semaphore(name))

        x_sb = sb("x_sb", [P, NBATCH * TILES, D])
        wqvk_sb = sb("wqvk_sb", [P, 3 * D])
        wo_sb = sb("wo_sb", [P, D])
        c_sb = sb("c_sb", [NBATCH, D])
        gate_sb = sb("gate_sb", [OPEN, D])
        ident = sb("ident", [P, P])
        ident_bf = sb("ident_bf", [P, P], bf16)
        causal_bf = sb("causal_bf", [P, 2, P], bf16)
        minus_half = sb("minus_half", [P, TILES])
        sel = sb("sel", [2 * OPEN, OPEN + PAIRS, P], fp32r)
        before = sb("before", [P, OPEN, OPEN])
        wqk_hi = sb("wqk_hi", [P, 2, GROUPS * P], fp32r)
        wqk_lo = sb("wqk_lo", [P, 2, GROUPS * P], fp32r)
        row_tmp = sb("row_tmp", [P, 2])
        low_q = sb("low_q", [P, 1])
        low_k = sb("low_k", [P, 1])
        minus_row = sb("minus_row", [P, GROUPS])
        cT = sb("cT", [P, NBATCH])
        gate_wT = sb("gate_wT", [P, OPEN])
        mod = sb("mod", [P, NMOD, NBATCH])
        wo_gated = sb("wo_gated", [P, NBATCH, D])
        w1_hi = sb("w1_hi", [P, UNITS, P], fp32r)
        w1_lo = sb("w1_lo", [P, UNITS, P], fp32r)
        w3_hi = sb("w3_hi", [P, UNITS, P], fp32r)
        w3_lo = sb("w3_lo", [P, UNITS, P], fp32r)
        w2_hi = sb("w2_hi", [P, UNITS, D], fp32r)
        w2_lo = sb("w2_lo", [P, UNITS, D], fp32r)
        stats = sb("stats", [P, 2, TILES, 6])
        mv = sb("mv", [P, 2, TILES, 2])
        veps = sb("veps", [P, 2, TILES])
        rstd = sb("rstd", [P, 2, TILES])
        xn = sb("xn", [P, 2, TILES, D])
        hT = sb("hT", [P, SEQ])
        hT_hi = sb("hT_hi", [P, SEQ], fp32r)
        hT_lo = sb("hT_lo", [P, SEQ], fp32r)
        cut = sb("cut", [P, 2, GROUPS, SEQ], fp32r)
        q_rows = sb("q_rows", [P, GROUPS, SEQ], fp32r)
        k_rows = sb("k_rows", [P, GROUPS, SEQ], fp32r)
        q_max = sb("q_max", [P, GROUPS, SEQ], fp32r)
        v_ones = sb("v_ones", [P, TILES, HEADS, STRIP])
        peak = sb("peak", [P, TILES, GROUP, STRIP])
        probs0 = sb("probs0", [P, 2, GROUP, SEQ])
        probs1 = sb("probs1", [P, 2, GROUP, P])
        oT = sb("oT", [P, GROUPS, SEQ])
        rden = sb("rden", [P, TILES, HEADS])
        attn = sb("attn", [P, TILES, HEADS, HD])
        attnT = sb("attnT", [P, SEQ])
        wqk_f = probs1[:].rearrange("p i g s -> p i (g s)")
        lmax = sb("lmax", [P, TILES])
        lshift = sb("lshift", [P, TILES, OPEN])
        prob = sb("prob", [P, TILES, OPEN])
        above = sb("above", [P, TILES, OPEN, OPEN])
        same = sb("same", [P, TILES, OPEN, OPEN])
        rank = sb("rank", [P, TILES, OPEN])
        kept = sb("kept", [P, TILES, OPEN])
        ksum = sb("ksum", [P, TILES])
        krec = sb("krec", [P, TILES])
        share = sb("share", [P, TILES, OPEN])
        share_cut = sb("share_cut", [P, TILES, 2 * OPEN], fp32r)
        x1 = x_sb
        h2 = sb("h2", [P, SEQ])
        h2T = sb("h2T", [P, NBATCH * SEQ])
        h2_hi = sb("h2_hi", [P, NBATCH * SEQ], fp32r)
        h2_lo = sb("h2_lo", [P, NBATCH * SEQ], fp32r)
        shareT = sb("shareT", [2 * OPEN, NBATCH * SEQ], fp32r)
        xw_hi = sb("xw_hi", [P, 2, SEQ], fp32r)
        xw_lo = sb("xw_lo", [P, 2, SEQ], fp32r)
        hid_hi = sb("hid_hi", [P, SLOTS, SEQ], fp32r)
        hid_lo = sb("hid_lo", [P, SLOTS, SEQ], fp32r)
        work = sb("work", [P, SLOTS + 8, SEQ])
        hid, th, glu = work[:, 0:SLOTS, :], work[:, SLOTS:SLOTS + 2, :], work[:, SLOTS + 2:SLOTS + 4, :]
        xw, pair_share, yT = (work[:, SLOTS + n, :] for n in (4, 5, 6))
        y_out = work[:, SLOTS + 7, :].rearrange("p (t d) -> p t d", t=TILES)
        w_raw = work[:].rearrange("p n c -> p (n c)")[:, 0:2 * UP * P].rearrange(
            "p (i u f) -> p i u f", i=2, f=P)
        wmod_sb = h2T[:, 0:NMOD * D]
        c_rows = oT[:].rearrange("p g s -> p (g s)").rearrange("p (b n) -> p b n", n=P)
        gsign = h2T[:, NMOD * D:(NMOD + NBATCH) * D].rearrange("p (b d) -> p b d", d=D)
        spare = h2T[:, NMOD * D:NBATCH * SEQ].rearrange("p (n d) -> p n d", d=D)
        sel_f = spare[0:2 * OPEN, 0:OPEN + PAIRS, :]
        c_exp, c_rec, c_silu = (spare[0:NBATCH, OPEN + PAIRS + n, :] for n in range(3))

        A = [ctx.enter_context(nc.psum_tensor(f"A{i}", [P, 2 * BANK], fp32)) for i in range(2)]
        T = ctx.enter_context(nc.psum_tensor("T", [P, BANK], fp32))
        G = ctx.enter_context(nc.psum_tensor("G", [P, BANK], fp32))
        U = ctx.enter_context(nc.psum_tensor("U", [P, BANK], fp32))
        Y = ctx.enter_context(nc.psum_tensor("Y", [P, BANK], fp32))

        x0_in = sem("x0_in")
        x_in = sem("x_in")
        attn_w_in = sem("attn_w_in")
        mod_in = sem("mod_in")
        w_in = [sem(f"w_in_{i}") for i in range(3 * PAIRS)]
        zeroed = sem("zeroed")
        pool_const = sem("pool_const")
        consts = sem("consts")
        wqk_step = sem("wqk_step")
        wqk_hi_ready = sem("wqk_hi_ready")
        wqk_ready = sem("wqk_ready")
        setup_dve = sem("setup_dve")
        setup_pe = sem("setup_pe")
        setup_act = sem("setup_act")
        w_cut_hi = sem("w_cut_hi")
        w_cut = sem("w_cut")
        a_written = sem("a_written")
        a_read = sem("a_read")
        t_written = sem("t_written")
        t_read = sem("t_read")
        gate_rows_ready = sem("gate_rows_ready")
        gate_spread = sem("gate_spread")
        gate_step = sem("gate_step")
        gate_folded = sem("gate_folded")
        first_q_max = sem("first_q_max")
        var_ready = sem("var_ready")
        rstd_ready = sem("rstd_ready")
        xn_ready = sem("xn_ready")
        masked = sem("masked")
        hi_ready = sem("hi_ready")
        lo_ready = sem("lo_ready")
        cut_ready = sem("cut_ready")
        prob_ready = sem("prob_ready")
        share_ready = sem("share_ready")
        dve_step = sem("dve_step")
        h2_hi_ready = sem("h2_hi_ready")
        h2_cut = sem("h2_cut")
        h2_kept = sem("h2_kept")
        xw_hi_ready = sem("xw_hi_ready")
        xw_cut = sem("xw_cut")
        g_written = sem("g_written")
        g_read = sem("g_read")
        u_written = sem("u_written")
        u_read = sem("u_read")
        tanh_done = sem("tanh_done")
        scaled = sem("scaled")
        hid_hi_ready = sem("hid_hi_ready")
        hid_cut = sem("hid_cut")
        down_done = sem("down_done")
        y_read = sem("y_read")
        out_sent = sem("out_sent")
        out_free = sem("out_free")
        waits_apart = sem("waits_apart")

        SETUP = 1
        N_A, N_T = 5 + 4 * GROUPS, 8 + GROUPS
        A_S, A_E, A_O = 4, 4 + 2 * GROUPS, 4 + 4 * GROUPS
        (T_XN, T_V, T_MAX), T_PV = range(3), 3
        T_ATTN, T_WO, T_H2, T_LOGIT, T_SHARE = range(3 + GROUPS, 8 + GROUPS)

        def expert_steps(lag):
            steps = [("gate", 0), ("share", 0), ("share", 1), ("share", OPEN)]
            for n in range(UNITS):
                if n == FULL + 1:
                    steps.append(("share", 2))
                if n == FULL + 4:
                    steps.append(("share", OPEN + 1))
                if n == UP + 1:
                    steps.append(("share", 3))
                if n + 1 < UNITS:
                    steps.append(("gate", n + 1))
                if n:
                    steps.append(("round", n - 1))
                steps.append(("up", n))
                if n >= lag:
                    steps.append(("down", n - lag))
            steps.append(("round", UNITS - 1))
            return steps + [("down", n) for n in range(UNITS - lag, UNITS)] + [("output", 0)]

        STEPS = expert_steps(LAG)
        U_USES = [step for step in STEPS if step[0] in ("share", "up", "output")]
        N_U = len(U_USES)

        def u_use(b, part, n):
            return b * N_U + U_USES.index((part, n)) + 1

        LEAD = 84
        PLACES = [
            (("stats1",), dict(V=0)),
            (("moments1",), dict(V=1)),
            (("norm1",), dict(V=3, G=2)),
            (("scale1",), dict(V=8)),
            (("xnT",), dict(T=9, V=10, S=8, G=9)),
            (("proj", 0, 0,), dict(T=13, S=13, V=13)),
            (("proj", 1, 0,), dict(T=13, S=13, V=14)),
            (("proj", 0, 1,), dict(T=14, S=14, V=14)),
            (("proj", 1, 1,), dict(T=16, S=16, V=17)),
            (("v",), dict(T=17, S=25)),
            (("scores", 0, 0,), dict(T=17, V=17)),
            (("scores", 0, 1,), dict(T=19, V=18)),
            (("scores", 1, 0,), dict(T=20, V=20)),
            (("scores", 1, 1,), dict(T=21, V=23)),
            (("scores", 2, 0,), dict(T=26, V=25)),
            (("scores", 2, 1,), dict(T=27, V=28)),
            (("scores", 3, 0,), dict(T=29, V=32)),
            (("scores", 3, 1,), dict(T=36, V=37)),
            (("peaks",), dict(T=41, V=41)),
            (("exps", 0, 0,), dict(T=44, S=43)),
            (("exps", 0, 1,), dict(T=46, S=47)),
            (("mask", 0,), dict(G=50)),
            (("exps", 1, 0,), dict(T=48, S=47)),
            (("exps", 1, 1,), dict(T=52, S=52)),
            (("mask", 1,), dict(G=53)),
            (("weigh", 0,), dict(T=54, S=53)),
            (("exps", 2, 0,), dict(T=56, S=56)),
            (("exps", 2, 1,), dict(T=56, S=58)),
            (("mask", 2,), dict(G=56)),
            (("weigh", 1,), dict(T=59, S=60)),
            (("exps", 3, 0,), dict(T=59, S=61)),
            (("exps", 3, 1,), dict(T=59, S=61)),
            (("mask", 3,), dict(G=62)),
            (("weigh", 2,), dict(T=65, S=61)),
            (("weigh", 3,), dict(T=67, S=66)),
            (("back",), dict(T=70, V=70)),
            (("attnT",), dict(T=73, S=73)),
            (("wo",), dict(T=75, V=75)),
            (("stats2",), dict(V=75)),
            (("moments2",), dict(V=75)),
            (("norm2",), dict(V=75, G=73)),
            (("scale2",), dict(V=78)),
            (("h2T",), dict(T=82, V=81, S=81, G=81)),
            (("logits",), dict(T=84, V=83, S=85)),
            (("above",), dict(V=84)),
            (("same",), dict(V=86)),
            (("beaten",), dict(V=87)),
            (("rank",), dict(V=87)),
            (("kept",), dict(V=88)),
            (("ksum",), dict(V=90)),
            (("krec",), dict(V=91)),
            (("share",), dict(V=91)),
            (("share_hi",), dict(V=91)),
            (("share_lo",), dict(V=91)),
            (("spread",), dict(T=95, V=95)),
        ]
        CUT_AFTER = {"S": [6, 7, 10, 12, 12, 15], "G": [5, 9, 11, 17, 20, 22]}
        FOLD_AFTER = ("weigh", 1,)
        ATTENTION, EXPERTS = "attention", "experts"
        TAIL = [(NBATCH - 2, step) for step in STEPS[LEAD:]]
        TAIL += [(NBATCH - 1, step) for step in expert_steps(TAIL_LAG)]

        def merged(letter):
            steps = [(EXPERTS, 1, step) for step in STEPS[LEAD:]] + [(EXPERTS, 0, step) for step in STEPS[:LEAD]]
            order = []
            for at in range(len(STEPS) + 1):
                order += [(ATTENTION, -1, step) for step, places in PLACES if places.get(letter) == at]
                order += steps[at:at + 1]
            return order

        def run(eng, letter, attention, experts, cut_weight=None, extra={}):
            for n, (step, places) in enumerate(PLACES):
                if letter in places:
                    attention(0, *step)
                if step in extra:
                    extra[step]()
                if cut_weight:
                    for i, place in enumerate(CUT_AFTER[letter]):
                        if place == n:
                            cut_weight(i)
            order = merged(letter)
            for part, back, step in order:
                if part == ATTENTION:
                    attention(1, *step)
                elif back == 0:
                    experts(0, *step)
            with eng.Fori(1, NBATCH - 1) as b:
                for part, back, step in order:
                    if part == ATTENTION:
                        attention(b + 1, *step)
                    else:
                        experts(b - back if back else b, *step)
            for b, step in TAIL:
                experts(b, *step, tail=True)

        TAIL_GATES = [(b, step[1]) for b, step in TAIL if step[0] == "gate"]
        TAIL_USES = [(b, step) for b, step in TAIL if step in U_USES]

        def g_bank(tail, b, n):
            at = TAIL_GATES.index((b, n)) if tail else 0
            return (A[0][:, 0:BANK] if at % 2 else G[:]), int(at > 0)

        def u_bank(tail, b, part, n):
            at = TAIL_USES.index((b, (part, n))) if tail else 0
            return (A[1][:, 0:BANK] if at % 2 else U[:]), int(at > 0)

        block = ctx.enter_context(nc.Block())

        def two_heads(n):
            return A[n % 2][:].rearrange("p (h i t) -> p h i t", h=2, i=TILES)

        def wait_apart(eng, s, value):
            eng.wait_ge(s, value)
            eng.sem_inc(waits_apart, 1)

        PIECES = [(name, pair) for pair in range(PAIRS) for name in ("w1", "w3", "w2")]
        W_CUTS = {"w1": (w1_hi, w1_lo), "w3": (w3_hi, w3_lo), "w2": (w2_hi, w2_lo)}

        def cuts_of(i):
            name, pair = PIECES[i]
            units = slice(pair * UP, (pair + 1) * UP)
            return (w_raw[:, i % 2, :, :], *(w[:, units, :] for w in W_CUTS[name]))

        @block.sync
        def _(sp):
            sp.dma_start(x_sb[:, 0:TILES, :],
                         h[0, :, :].rearrange("(t p) d -> p t d", p=P)).then_inc(x0_in, 16)
            sp.dma_start(wqvk_sb[:], wqvk).then_inc(attn_w_in, 16)
            sp.dma_start(wo_sb[:], wo).then_inc(attn_w_in, 16)
            sp.dma_start(x_sb[:, TILES:, :], h[1:, :, :].rearrange("b (t p) d -> p (b t) d", p=P)
                         ).then_inc(x_in, 16)
            for i, (name, pair) in enumerate(PIECES):
                e, raw, s = 2 * pair, w_raw[:, i % 2, :, :], w_in[i]
                if i >= 2:
                    sp.wait_ge(w_cut, i - 1)
                if name == "w2":
                    sp.dma_start(raw[:, 0:FULL, :],
                                 w2[e, 0:FULL * P, :].rearrange("(u p) d -> p u d", p=P)).then_inc(s, 16)
                    sp.dma_start(raw[0:HALF, FULL, :], w2[e, FULL * P:HID, :]).then_inc(s, 16)
                    sp.dma_start(raw[HALF:P, FULL, :], w2[e + 1, FULL * P:HID, :]).then_inc(s, 16)
                    sp.dma_start(raw[:, FULL + 1:UP, :],
                                 w2[e + 1, 0:FULL * P, :].rearrange("(u p) d -> p u d", p=P)).then_inc(s, 16)
                else:
                    w = {"w1": w1, "w3": w3}[name]
                    flat = raw.rearrange("p u f -> p (u f)")
                    sp.dma_start(flat[:, 0:HID], w[e, :, :]).then_inc(s, 16)
                    sp.dma_start(flat[:, HID:HID + HALF], w[e + 1, :, FULL * P:HID]).then_inc(s, 16)
                    sp.dma_start(flat[:, HID + HALF:2 * HID], w[e + 1, :, 0:FULL * P]).then_inc(s, 16)
            sp.sem_inc(out_free, 1)
            with sp.Fori(0, NBATCH) as b:
                sp.wait_ge(u_read, SETUP + b * N_U + N_U)
                sp.dma_start(out[bass.ds(b, 1), :, :].rearrange("b (t p) d -> p (b t) d", p=P),
                             y_out).then_inc(out_sent, 16)
                sp.wait_ge(out_sent, 16 * b + 16)
                sp.sem_inc(out_free, 1)

        def piece_in(i):
            return 16 * (4 if PIECES[i][0] == "w2" else 3)

        @block.gpsimd
        def _(pool):
            nc.gpsimd.memset(wqk_f, 0.0).then_inc(zeroed, 1)
            nc.gpsimd.memset(ident[:], 0.0).then_inc(pool_const, 1)
            nc.gpsimd.memset(causal_bf[:], 0.0).then_inc(pool_const, 1)
            nc.gpsimd.memset(sel_f, 0.0).then_inc(pool_const, 1)
            nc.gpsimd.memset(before[:], 1.0).then_inc(pool_const, 1)
            nc.gpsimd.memset(minus_half[:], -0.5).then_inc(consts, 1)
            pool.wait_ge(pool_const, 4)
            nc.gpsimd.affine_select(out=ident[:], in_=ident[:], compare_op=ALU.not_equal, fill=1.0, base=0,
                                    pattern=[[-1, P]], channel_multiplier=1).then_inc(consts, 1)
            nc.gpsimd.affine_select(out=causal_bf[:], in_=causal_bf[:], compare_op=ALU.is_ge, fill=MASKED,
                                    base=0, pattern=[[0, 2], [-1, P]], channel_multiplier=1).then_inc(consts, 1)
            nc.gpsimd.affine_select(out=before[:], in_=before[:], compare_op=ALU.is_ge, fill=0.0, base=-1,
                                    pattern=[[1, OPEN], [-1, OPEN]], channel_multiplier=0).then_inc(consts, 1)
            for n, base in enumerate((0, -OPEN)):
                if n:
                    pool.wait_ge(pool_const, 6)
                nc.gpsimd.affine_select(out=sel_f[:, 0:OPEN, :], in_=sel_f[:, 0:OPEN, :],
                                        compare_op=ALU.not_equal, fill=1.0, base=base,
                                        pattern=[[-1, OPEN], [0, P]], channel_multiplier=1
                                        ).then_inc(pool_const, 1)
                halves = sel_f[:, OPEN:, :].rearrange("p m (s f) -> p m s f", s=2)
                nc.gpsimd.affine_select(out=halves, in_=halves, compare_op=ALU.not_equal, fill=1.0,
                                        base=base, pattern=[[-2, PAIRS], [-1, 2], [0, HALF]],
                                        channel_multiplier=1).then_inc(pool_const, 1)
            nc.gpsimd.memset(v_ones[:], 0.0).then_inc(zeroed, 1)
            nc.gpsimd.memset(peak[:], 0.0).then_inc(zeroed, 1)
            pool.wait_ge(wqk_hi_ready, 1)
            nc.gpsimd.tensor_tensor(wqk_lo[:], wqk_f, wqk_hi[:].bitcast(fp32),
                                    ALU.subtract).then_inc(wqk_ready, 1)

            def left(out, value, hi):
                return nc.gpsimd.tensor_tensor(out, value, hi.bitcast(fp32), ALU.subtract)

            def attention(b, part, *at):
                if part in ("norm1", "norm2"):
                    k = int(part == "norm2")
                    pool.wait_ge(var_ready, b * 2 + k + 1)
                    nc.gpsimd.tensor_tensor(rstd[:, k, :], veps[:, k, :], minus_half[:],
                                            ALU.pow).then_inc(rstd_ready, 1)
                elif part == "xnT":
                    pool.wait_ge(hi_ready, b + 1)
                    left(hT_lo[:], hT[:], hT_hi[:]).then_inc(lo_ready, 1)
                elif part == "mask":
                    g, = at
                    wait_apart(pool, a_read, SETUP + b * N_A + A_E + 2 * g + 2)
                    for pr in (probs0, probs1):
                        band = pr[:, g % 2, :, 0:P]
                        nc.gpsimd.affine_select(out=band, in_=band, compare_op=ALU.is_ge, fill=0.0, base=0,
                                                pattern=[[0, GROUP], [1, P]], channel_multiplier=-1
                                                ).then_inc(masked, 1)
                elif part == "h2T":
                    pool.wait_ge(h2_hi_ready, b + 1)
                    left(h2_lo[:, bass.ds(b * SEQ, SEQ)], h2[:],
                         h2_hi[:, bass.ds(b * SEQ, SEQ)]).then_inc(h2_cut, 1)

            def experts(b, part, n, tail=False):
                if part == "share" and n < OPEN:
                    pool.wait_ge(xw_hi_ready, b * OPEN + n + 1)
                    left(xw_lo[:, n % 2, :], xw, xw_hi[:, n % 2, :]).then_inc(xw_cut, 1)
                elif part == "round":
                    slot = n % SLOTS
                    pool.wait_ge(hid_hi_ready, b * UNITS + n + 1)
                    left(hid_lo[:, slot, :], hid[:, slot, :], hid_hi[:, slot, :]).then_inc(hid_cut, 1)

            def cut_weight(i):
                raw, hi, lo = cuts_of(i)
                pool.wait_ge(w_cut_hi, i + 1)
                left(lo, raw, hi).then_inc(w_cut, 1)

            run(pool, "G", attention, experts, cut_weight)

        @block.scalar
        def _(act):
            act.dma_start(c_sb[:], c).then_inc(mod_in, 16)
            act.dma_start(gate_sb[:], gate_w[0:OPEN, :]).then_inc(mod_in, 16)
            act.dma_start(wmod_sb, wmod).then_inc(mod_in, 16)
            act.wait_ge(mod_in, 48)
            nc.scalar.activation(c_exp, c_sb[:], ACT.Exp, scale=-1.0).then_inc(setup_act, 1)
            act.wait_ge(wqk_step, 1)
            nc.scalar.activation(wqk_hi[:], wqk_f, ACT.Copy).then_inc(wqk_hi_ready, 1)

            def attention(b, part, *at):
                if part == "xnT":
                    act.wait_ge(t_read, SETUP + b * N_T + T_XN + 1)
                    nc.scalar.activation(hT_hi[:], hT[:], ACT.Copy).then_inc(hi_ready, 1)
                elif part == "proj":
                    n, half = at
                    act.wait_ge(a_written, b * N_A + 2 * half + n + 1)
                    if n == 0:
                        nc.scalar.activation(cut[:, n, 2 * half:2 * half + 2, :],
                                             A[n][:, half * BANK:(half + 1) * BANK].rearrange(
                                                 "p (g s) -> p g s", g=2), ACT.Copy).then_inc(cut_ready, 1)
                    else:
                        for g in (2 * half, 2 * half + 1):
                            last = nc.scalar.activation(cut[:, n, g, :], A[n][:, g * SEQ:(g + 1) * SEQ],
                                                        ACT.Identity, bias=minus_row[:, g:g + 1])
                        last.then_inc(cut_ready, 1)
                elif part == "v":
                    act.wait_ge(t_written, b * N_T + T_V + 1)
                    nc.scalar.activation(v_ones[:, :, :, 0:HD].rearrange("p t h d -> p (t h) d"),
                                         T[:, 0:SEQ].rearrange("p (n d) -> p n d", d=HD),
                                         ACT.Copy).then_inc(t_read, 1)
                elif part == "exps":
                    g, hp = at
                    n = A_E + 2 * g + hp
                    act.wait_ge(a_written, b * N_A + n + 1)
                    if g >= 2 and hp == 0:
                        act.wait_ge(t_written, b * N_T + T_PV + g - 1)
                    s, heads = two_heads(n), slice(2 * hp, 2 * hp + 2)
                    nc.scalar.activation(probs0[:, g % 2, heads, :], s[:, :, 0, :], ACT.Exp,
                                         scale=SCORE_SCALE)
                    nc.scalar.activation(probs1[:, g % 2, heads, :], s[:, :, 1, P:SEQ], ACT.Exp,
                                         scale=SCORE_SCALE).then_inc(a_read, 1)
                elif part == "weigh":
                    g, = at
                    act.wait_ge(t_written, b * N_T + T_PV + g + 1)
                    nc.scalar.activation(oT[:, g, :], T[:, 0:SEQ], ACT.Copy).then_inc(t_read, 1)
                elif part == "attnT":
                    act.wait_ge(t_written, b * N_T + T_ATTN + 1)
                    nc.scalar.activation(attnT[:], T[:, 0:SEQ], ACT.Copy).then_inc(t_read, 1)
                elif part == "h2T":
                    act.wait_ge(t_read, SETUP + b * N_T + T_H2 + 1)
                    nc.scalar.activation(h2_hi[:, bass.ds(b * SEQ, SEQ)], h2[:],
                                         ACT.Copy).then_inc(h2_hi_ready, 1)
                    nc.scalar.activation(h2T[:, bass.ds(b * SEQ, SEQ)], h2[:], ACT.Copy).then_inc(h2_kept, 1)
                elif part == "logits":
                    act.wait_ge(t_read, SETUP + b * N_T + T_LOGIT + 1)
                    nc.scalar.activation(prob[:], lshift[:], ACT.Exp).then_inc(prob_ready, 1)

            def experts(b, part, n, tail=False):
                if part == "share":
                    use = u_use(b, part, n)
                    if n < OPEN:
                        act.wait_ge(u_read, SETUP + use)
                        if n >= 2:
                            act.wait_ge(u_written, SETUP + u_use(b, "up", FULL - 1 if n == 2 else UP - 1))
                        nc.scalar.activation(xw_hi[:, n % 2, :], xw, ACT.Copy).then_inc(xw_hi_ready, 1)
                    else:
                        act.wait_ge(u_written, SETUP + use)
                        if tail:
                            act.wait_ge(u_read, SETUP + use - 1)
                        nc.scalar.activation(pair_share, u_bank(tail, b, part, n)[0][:, 0:SEQ],
                                             ACT.Copy).then_inc(u_read, 1)
                elif part == "gate":
                    act.wait_ge(g_written, b * UNITS + n + 1)
                    nc.scalar.activation(th[:, n % 2, :], g_bank(tail, b, n)[0][:, 0:SEQ], ACT.Tanh,
                                         scale=0.5).then_inc(tanh_done, 1)
                elif part == "round":
                    act.wait_ge(u_read, SETUP + u_use(b, "up", n))
                    if n % UP == FULL:
                        act.wait_ge(scaled, b * PAIRS + n // UP + 1)
                    if n >= SLOTS:
                        act.wait_ge(down_done, b * UNITS + n - SLOTS + 1)
                    nc.scalar.activation(hid_hi[:, n % SLOTS, :], hid[:, n % SLOTS, :],
                                         ACT.Copy).then_inc(hid_hi_ready, 1)

            def cut_weight(i):
                raw, hi, _ = cuts_of(i)
                act.wait_ge(w_in[i], piece_in(i))
                nc.scalar.activation(hi, raw, ACT.Copy).then_inc(w_cut_hi, 1)

            run(act, "S", attention, experts, cut_weight)

        @block.tensor
        def _(pe):
            def cut_product(dst, w_hi, w_lo, x_hi, x_lo, start=True, stop=True):
                nc.tensor.matmul(dst, w_hi, x_hi, start=start, stop=False)
                nc.tensor.matmul(dst, w_hi, x_lo, start=False, stop=False)
                return nc.tensor.matmul(dst, w_lo, x_hi, start=False, stop=stop)

            pe.wait_ge(consts, 4)
            pe.wait_ge(mod_in, 48)
            nc.tensor.transpose(T[:, 0:OPEN], gate_sb[:], ident[0:OPEN, 0:OPEN]).then_inc(setup_pe, 1)
            pe.wait_ge(setup_dve, 3)
            nc.tensor.transpose(G[:, 0:NBATCH], c_silu, ident[0:NBATCH, 0:NBATCH]).then_inc(setup_pe, 1)
            pe.wait_ge(g_read, SETUP)
            for m in range(NMOD):
                last = nc.tensor.matmul(U[:, m * NBATCH:(m + 1) * NBATCH], wmod_sb[:, m * D:(m + 1) * D],
                                        cT[:], start=True, stop=True)
            last.then_inc(u_written, 1)

            def spread_gates():
                pe.wait_ge(gate_rows_ready, 1)
                for b in range(NBATCH):
                    last = nc.tensor.matmul((G, Y)[2 * b // NBATCH][:, b % (NBATCH // 2) * D:][:, 0:D],
                                            c_rows[:, b, :], wmod_sb[:, 2 * D:3 * D], start=True, stop=True)
                last.then_inc(gate_spread, 1)

            def attention(b, part, *at):
                def t_free(n):
                    pe.wait_ge(t_read, SETUP + b * N_T + n)

                def a_free(n):
                    pe.wait_ge(a_read, SETUP + b * N_A + max(n - 1, 0))

                def transposed(src, t):
                    for i in range(TILES):
                        last = nc.tensor.transpose(T[:, i * P:(i + 1) * P], src(i), ident[:])
                    last.then_inc(t_written, 1)

                if part == "xnT":
                    pe.wait_ge(xn_ready, b * 2 + 1)
                    t_free(T_XN)
                    transposed(lambda i: xn[:, 0, i, :], T_XN)
                elif part == "proj":
                    pe.wait_ge(lo_ready, b + 1)
                    pe.wait_ge(wqk_ready, 1)
                    n, half = at
                    a_free(0)
                    for g in (2 * half, 2 * half + 1):
                        cols = slice(g * P, (g + 1) * P)
                        last = cut_product(A[n][:, g * SEQ:(g + 1) * SEQ], wqk_hi[:, n, cols],
                                           wqk_lo[:, n, cols], hT_hi[:], hT_lo[:])
                    last.then_inc(a_written, 1)
                elif part == "v":
                    t_free(T_V)
                    for i in range(TILES):
                        last = nc.tensor.matmul(T[:, i * P:(i + 1) * P], hT[:, i * P:(i + 1) * P],
                                                wqvk_sb[:, D:2 * D], start=True, stop=True)
                    last.then_inc(t_written, 1)
                elif part == "scores":
                    g, hp = at
                    n = A_S + 2 * g + hp
                    a_free(n)
                    dst = two_heads(n)
                    for k in range(2):
                        blocks = dst[:, k, :, :].rearrange("p i t -> p (i t)").rearrange(
                            "p (n t) -> p n t", t=P)
                        nc.tensor.matmul(blocks[:, 0:4:3, :], ident_bf[:], causal_bf[:], start=True, stop=True)
                    for i in range(TILES):
                        for k in range(2):
                            rows = slice((2 * hp + k) * STRIP, (2 * hp + k + 1) * STRIP)
                            last = nc.tensor.matmul(dst[:, k, i, :], q_rows[rows, g, i * P:(i + 1) * P],
                                                    k_rows[rows, g, :], start=False, stop=True,
                                                    skip_group_check=True)
                    last.then_inc(a_written, 1)
                elif part == "peaks":
                    pe.wait_ge(a_read, SETUP + b * N_A + A_E)
                    t_free(T_MAX)
                    transposed(lambda i: peak[:, i, :, :].rearrange("p j r -> p (j r)"), T_MAX)
                elif part == "exps":
                    g, hp = at
                    n = A_E + 2 * g + hp
                    if n == A_E:
                        pe.wait_ge(first_q_max, b + 1)
                    elif g == 2 and hp == 0:
                        t_free(T_MAX + 1)
                    a_free(n)
                    dst = two_heads(n)
                    for i in range(TILES):
                        for k in range(2):
                            rows = slice((2 * hp + k) * STRIP, (2 * hp + k + 1) * STRIP)
                            last = nc.tensor.matmul(dst[:, k, i, :], k_rows[rows, g, i * P:(i + 1) * P],
                                                    q_max[rows, g, :], start=i == 0, stop=True,
                                                    skip_group_check=True)
                    last.then_inc(a_written, 1)
                elif part == "weigh":
                    g, = at
                    t_free(T_PV + g)
                    pe.wait_ge(masked, b * 2 * GROUPS + 2 * g + 2)
                    for j in range(GROUP):
                        nc.tensor.matmul(T[j * STRIP:(j + 1) * STRIP, 0:SEQ], v_ones[:, 0, g * GROUP + j, :],
                                         probs0[:, g % 2, j, :], start=True, stop=False)
                    for j in range(GROUP):
                        last = nc.tensor.matmul(T[j * STRIP:(j + 1) * STRIP, P:SEQ],
                                                v_ones[:, 1, g * GROUP + j, :], probs1[:, g % 2, j, :],
                                                start=False, stop=True)
                    last.then_inc(t_written, 1)
                elif part == "back":
                    a_free(A_O)
                    t_free(T_ATTN)
                    for i in range(TILES):
                        for g in range(GROUPS):
                            last = nc.tensor.transpose(A[0][:, i * BANK + g * P:i * BANK + (g + 1) * P],
                                                       oT[:, g, i * P:(i + 1) * P], ident[:])
                    last.then_inc(a_written, 1)
                elif part == "attnT":
                    pe.wait_ge(a_read, SETUP + b * N_A + N_A)
                    transposed(lambda i: attn[:, i, :, :].rearrange("p h d -> p (h d)"), T_ATTN)
                elif part == "wo":
                    t_free(T_WO)
                    pe.wait_ge(gate_folded, 1)
                    for i in range(TILES):
                        last = nc.tensor.matmul(T[:, i * D:(i + 1) * D], attnT[:, i * P:(i + 1) * P],
                                                wo_gated[:, bass.ds(b, 1), :].rearrange("p a d -> p (a d)"),
                                                start=True, stop=True)
                    last.then_inc(t_written, 1)
                elif part == "h2T":
                    pe.wait_ge(xn_ready, b * 2 + 2)
                    transposed(lambda i: xn[:, 1, i, :], T_H2)
                elif part == "logits":
                    t_free(T_LOGIT)
                    for i in range(TILES):
                        last = nc.tensor.matmul(T[:, i * OPEN:(i + 1) * OPEN], h2[:, i * P:(i + 1) * P],
                                                gate_wT[:], start=True, stop=True)
                    last.then_inc(t_written, 1)
                elif part == "spread":
                    pe.wait_ge(share_ready, b + 1)
                    for i in range(TILES):
                        last = nc.tensor.transpose(T[0:2 * OPEN, i * P:(i + 1) * P],
                                                   share_cut[:, i, :].bitcast(fp32), ident[:])
                    last.then_inc(t_written, 1)

            def experts(b, part, n, tail=False):
                tokens = bass.ds(b * SEQ, SEQ)
                if part == "gate":
                    bank, outstanding = g_bank(tail, b, n)
                    if n == 0:
                        pe.wait_ge(h2_cut, b + 1)
                        pe.wait_ge(w_cut, len(PIECES))
                    pe.wait_ge(g_read, SETUP + b * UNITS + n - outstanding)
                    cut_product(bank[:, 0:SEQ], w1_hi[:, n, :], w1_lo[:, n, :], h2_hi[:, tokens],
                                h2_lo[:, tokens]).then_inc(g_written, 1)
                elif part == "down":
                    pe.wait_ge(hid_cut, b * UNITS + n + 1)
                    cut_product(Y[:, 0:SEQ], w2_hi[:, n, :], w2_lo[:, n, :], hid_hi[:, n % SLOTS, :],
                                hid_lo[:, n % SLOTS, :], start=n == 0, stop=n == UNITS - 1
                                ).then_inc(down_done, 1)
                elif part in ("share", "up", "output"):
                    bank, outstanding = u_bank(tail, b, part, n)
                    free = SETUP + u_use(b, part, n) - 1 - outstanding
                    if part == "share":
                        if n == 0:
                            pe.wait_ge(t_read, SETUP + b * N_T + N_T)
                        wait_apart(pe, u_read, free)
                        last = nc.tensor.matmul(bank[:, 0:SEQ], sel[:, n, :], shareT[:, tokens], start=True,
                                                stop=True)
                    elif part == "up":
                        s = expert_of(n % UP)
                        if n % UP in (0, FULL + 1):
                            pe.wait_ge(xw_cut, b * OPEN + 2 * (n // UP) + s + 1)
                        pe.wait_ge(u_read, free)
                        xs = (h2_hi[:, tokens], h2_lo[:, tokens]) if s is None else \
                            (xw_hi[:, s, :], xw_lo[:, s, :])
                        last = cut_product(bank[:, 0:SEQ], w3_hi[:, n, :], w3_lo[:, n, :], *xs)
                    else:
                        pe.wait_ge(u_read, free)
                        pe.wait_ge(y_read, b + 1)
                        for i in range(TILES):
                            last = nc.tensor.transpose(bank[:, i * P:(i + 1) * P], yT[:, i * P:(i + 1) * P],
                                                       ident[:])
                    last.then_inc(u_written, 1)

            run(pe, "T", attention, experts, extra={("peaks",): spread_gates})

        @block.vector
        def _(dve):
            done = [0]

            def setup(ins):
                done[0] += 1
                ins.then_inc(setup_dve, 1)
                dve.wait_ge(setup_dve, done[0])

            dve.wait_ge(zeroed, 1)
            dve.wait_ge(attn_w_in, 32)
            for n, at in ((0, 0), (1, 2 * D)):
                dst = wqk_f[:, n, :].rearrange("p (h r) -> p h r", r=STRIP)
                for r in range(REP):
                    last = nc.vector.tensor_copy(dst[:, :, r * HD:(r + 1) * HD],
                                                 wqvk_sb[:, at:at + D].rearrange("p (h d) -> p h d", d=HD))
            last.then_inc(wqk_step, 1)
            dve.wait_ge(setup_act, 1)
            setup(nc.vector.tensor_scalar_add(c_exp, c_exp, 1.0))
            setup(nc.vector.reciprocal(c_rec, c_exp))
            setup(nc.vector.tensor_tensor(c_silu, c_sb[:], c_rec, ALU.mult))
            dve.wait_ge(setup_pe, 1)
            nc.vector.tensor_copy(gate_wT[:], T[:, 0:OPEN]).then_inc(t_read, 1)
            dve.wait_ge(setup_pe, 2)
            nc.vector.tensor_copy(cT[:], G[:, 0:NBATCH]).then_inc(g_read, 1)
            dve.sem_inc(a_read, SETUP)
            dve.wait_ge(consts, 4)
            nc.vector.tensor_copy(ident_bf[:], ident[:])
            id_rows = ident[:].rearrange("p (j r) -> p j r", r=STRIP)
            nc.vector.tensor_reduce(low_q[:], id_rows[:, :, 2 * HD:3 * HD], AX.XY, ALU.add, negate=True)
            nc.vector.tensor_reduce(row_tmp[:, 0:1], id_rows[:, :, HD:2 * HD], AX.XY, ALU.add)
            nc.vector.tensor_reduce(row_tmp[:, 1:2], id_rows[:, :, REP * HD:REP * HD + GROUPS], AX.XY, ALU.add)
            setup(nc.vector.tensor_reduce(minus_row[:], id_rows[:, :, REP * HD:REP * HD + GROUPS].rearrange(
                "p j g -> p g j"), AX.X, ALU.add, negate=True))
            nc.vector.tensor_tensor(low_k[:], row_tmp[:, 1:2], row_tmp[:, 0:1],
                                    ALU.subtract).then_inc(wqk_step, 1)
            dve.wait_ge(wqk_step, 2)
            m_ps = U[:, 0:NMOD * NBATCH].rearrange("p (m b) -> p m b", m=NMOD)

            def modulate():
                dve.wait_ge(u_written, SETUP)
                nc.vector.tensor_copy(mod[:, 0, :], m_ps[:, 0, :])
                nc.vector.tensor_scalar_add(mod[:, 1, :], m_ps[:, 1, :], 1.0)
                nc.vector.tensor_copy(mod[:, 3, :], m_ps[:, 3, :])
                nc.vector.tensor_scalar_add(mod[:, 4, :], m_ps[:, 4, :], 1.0)
                nc.vector.tensor_copy(mod[:, 5, :], m_ps[:, 5, :]).then_inc(u_read, 1)
                dve.wait_ge(u_read, SETUP)

            def repeat_c():
                dve.wait_ge(zeroed, 3)
                dve.wait_ge(pool_const, 8)
                nc.vector.memset(v_ones[:, :, :, HD:HD + 1], 1.0)
                nc.vector.tensor_copy(sel[:], sel_f).then_inc(wqk_step, 1)
                dve.wait_ge(g_read, SETUP)
                nc.vector.tensor_copy(c_rows, cT[:].unsqueeze(2).to_broadcast([P, NBATCH, P])
                                      ).then_inc(gate_rows_ready, 1)

            def fold_gates():
                steps = [0]

                def then(ins):
                    steps[0] += 1
                    ins.then_inc(gate_step, 1)
                    dve.wait_ge(gate_step, steps[0])

                def clamp(g, sign):
                    then(nc.vector.tensor_scalar(sign, g, 0.0, 2.0, ALU.is_ge, ALU.mult))
                    then(nc.vector.tensor_scalar_add(sign, sign, -1.0))
                    then(nc.vector.scalar_tensor_tensor(out=g, in0=g, scalar=-1.0, in1=g,
                                                        op0=ALU.mult, op1=ALU.max))
                    then(nc.vector.scalar_tensor_tensor(out=g, in0=g, scalar=GATE_FLOOR, in1=sign,
                                                        op0=ALU.max, op1=ALU.mult))

                dve.wait_ge(gate_spread, 1)
                half = NBATCH // 2
                nc.vector.tensor_copy(wo_gated[:, 0:half, :], G[:].rearrange("p (b d) -> p b d", d=D))
                then(nc.vector.tensor_copy(wo_gated[:, half:, :], Y[:].rearrange("p (b d) -> p b d", d=D)))
                clamp(wo_gated[:], gsign)
                clamp(mod[:, 5, :], gsign[:, 0, 0:NBATCH])
                nc.vector.tensor_tensor(wo_gated[:], wo_gated[:], wo_sb[:].unsqueeze(1).to_broadcast([P, NBATCH, D]),
                                        ALU.mult).then_inc(gate_folded, 1)

            DVE_STEPS = 15
            step = [0]
            square = [P, TILES, OPEN, OPEN]
            other = prob[:].unsqueeze(2).to_broadcast(square)
            own = prob[:].unsqueeze(3).to_broadcast(square)

            def attention(b, part, *at):
                if part == "stats1":
                    step[0] = 0

                def then(ins):
                    step[0] += 1
                    ins.then_inc(dve_step, 1)

                def ready():
                    wait_apart(dve, dve_step, b * DVE_STEPS + step[0])

                def t_wait(n):
                    dve.wait_ge(t_written, b * N_T + n + 1)

                def stats_of(src, k):
                    for i in range(TILES):
                        ins = nc.vector.bn_stats(stats[:, k, i, :], src[:, bass.ds(b * TILES + i, 1), :]
                                                 .rearrange("p a d -> p (a d)"))
                    then(ins)

                def moments(k):
                    ready()
                    for i in range(TILES):
                        ins = nc.vector.bn_aggr(mv[:, k, i, :], stats[:, k, i, :])
                    then(ins)

                def deviation(k):
                    ready()
                    nc.vector.tensor_scalar_add(veps[:, k, :], mv[:, k, :, 1], LN_EPS).then_inc(var_ready, 1)

                def scale(src, k):
                    dve.wait_ge(rstd_ready, b * 2 + k + 1)
                    for i in range(TILES):
                        ins = nc.vector.tensor_scalar(
                            xn[:, k, i, :], src[:, bass.ds(b * TILES + i, 1), :].rearrange("p a d -> p (a d)"),
                            mv[:, k, i, 0:1], rstd[:, k, i:i + 1], ALU.subtract, ALU.mult)
                    ins.then_inc(xn_ready, 1)

                if part == "stats1":
                    if isinstance(b, int) and b == 1:
                        dve.wait_ge(x_in, 16)
                    stats_of(x_sb, 0)
                elif part in ("moments1", "moments2"):
                    moments(int(part == "moments2"))
                elif part in ("norm1", "norm2"):
                    deviation(int(part == "norm2"))
                elif part == "scale1":
                    scale(x_sb, 0)
                elif part == "xnT":
                    t_wait(T_XN)
                    nc.vector.tensor_scalar(hT[:], T[:, 0:SEQ], mod[:, 1, bass.ds(b, 1)],
                                            mod[:, 0, bass.ds(b, 1)], ALU.mult, ALU.add).then_inc(t_read, 1)
                elif part == "proj":
                    n, half = at
                    rows, low = ((q_rows, low_q), (k_rows, low_k))[n]
                    dve.wait_ge(cut_ready, b * 4 + 2 * half + n + 1)
                    groups = slice(2 * half, 2 * half + 2)
                    nc.vector.scalar_tensor_tensor(
                        out=rows[:, groups, :].rearrange("p g s -> p (g s)"),
                        in0=cut[:, n, groups, :].rearrange("p g s -> p (g s)").bitcast(fp32),
                        scalar=low[:, 0:1], in1=A[n][:, half * BANK:(half + 1) * BANK],
                        op0=ALU.mult, op1=ALU.add).then_inc(a_read, 1)
                elif part == "scores":
                    g, hp = at
                    n = A_S + 2 * g + hp
                    dve.wait_ge(a_written, b * N_A + n + 1)
                    for i in range(TILES):
                        ins = nc.vector.reduce_max(peak[:, i, 2 * hp:2 * hp + 2, REP * HD + g],
                                                   two_heads(n)[:, :, i, 0:(i + 1) * P], AX.X)
                    ins.then_inc(a_read, 1)
                elif part == "peaks":
                    t_wait(T_MAX)
                    for groups, s in ((slice(0, 2), first_q_max), (slice(2, 4), t_read)):
                        nc.vector.tensor_tensor(q_max[:, groups, :], q_rows[:, groups, :].bitcast(fp32),
                                                T[:, 0:SEQ].unsqueeze(1).to_broadcast([P, 2, SEQ]),
                                                ALU.add).then_inc(s, 1)
                elif part == "back":
                    dve.wait_ge(a_written, b * N_A + A_O + 1)
                    sums = A[0][:].rearrange("p (t h r) -> p t h r", t=TILES, r=STRIP)
                    then(nc.vector.reciprocal(rden[:], sums[:, :, :, HD]))
                    ready()
                    nc.vector.tensor_tensor(attn[:], sums[:, :, :, 0:HD],
                                            rden[:].unsqueeze(3).to_broadcast([P, TILES, HEADS, HD]),
                                            ALU.mult).then_inc(a_read, 1)
                elif part == "wo":
                    t_wait(T_WO)
                    tiles = bass.ds(b * TILES, TILES)
                    nc.vector.tensor_tensor(x1[:, tiles, :], x_sb[:, tiles, :],
                                            T[:, 0:SEQ].rearrange("p (t d) -> p t d", t=TILES),
                                            ALU.add).then_inc(t_read, 1)
                elif part == "stats2":
                    wait_apart(dve, t_read, SETUP + b * N_T + T_WO + 1)
                    stats_of(x1, 1)
                elif part == "scale2":
                    scale(x1, 1)
                elif part == "h2T":
                    t_wait(T_H2)
                    nc.vector.tensor_scalar(h2[:], T[:, 0:SEQ], mod[:, 4, bass.ds(b, 1)],
                                            mod[:, 3, bass.ds(b, 1)], ALU.mult, ALU.add).then_inc(t_read, 1)
                elif part == "logits":
                    t_wait(T_LOGIT)
                    logits = T[:, 0:TILES * OPEN].rearrange("p (t e) -> p t e", e=OPEN)
                    then(nc.vector.reduce_max(lmax[:], logits, AX.X))
                    ready()
                    nc.vector.tensor_tensor(lshift[:], logits,
                                            lmax[:].unsqueeze(2).to_broadcast([P, TILES, OPEN]),
                                            ALU.subtract).then_inc(t_read, 1)
                elif part == "above":
                    dve.wait_ge(prob_ready, b + 1)
                    nc.vector.tensor_tensor(above[:], other, own, ALU.is_gt)
                    then(nc.vector.tensor_tensor(same[:], other, own, ALU.is_equal))
                elif part == "same":
                    ready()
                    then(nc.vector.tensor_tensor(same[:], same[:], before[:].unsqueeze(1).to_broadcast(square),
                                                 ALU.mult))
                elif part == "beaten":
                    ready()
                    then(nc.vector.tensor_tensor(above[:], above[:], same[:], ALU.add))
                elif part == "rank":
                    ready()
                    then(nc.vector.reduce_sum(rank[:], above[:], AX.X))
                elif part == "kept":
                    ready()
                    then(nc.vector.scalar_tensor_tensor(out=kept[:], in0=rank[:], scalar=2.0, in1=prob[:],
                                                        op0=ALU.is_lt, op1=ALU.mult))
                elif part == "ksum":
                    ready()
                    then(nc.vector.reduce_sum(ksum[:], kept[:], AX.X))
                elif part == "krec":
                    ready()
                    then(nc.vector.reciprocal(krec[:], ksum[:]))
                elif part == "share":
                    ready()
                    then(nc.vector.scalar_tensor_tensor(out=share[:], in0=kept[:], scalar=0.5,
                                                        in1=krec[:].unsqueeze(2).to_broadcast([P, TILES, OPEN]),
                                                        op0=ALU.mult, op1=ALU.mult))
                elif part == "share_hi":
                    ready()
                    then(nc.vector.tensor_copy(share_cut[:, :, 0:OPEN], share[:]))
                elif part == "share_lo":
                    ready()
                    nc.vector.tensor_tensor(share_cut[:, :, OPEN:], share[:],
                                            share_cut[:, :, 0:OPEN].bitcast(fp32),
                                            ALU.subtract).then_inc(share_ready, 1)
                elif part == "spread":
                    t_wait(T_SHARE)
                    nc.vector.tensor_copy(shareT[:, bass.ds(b * SEQ, SEQ)],
                                          T[0:2 * OPEN, 0:SEQ]).then_inc(t_read, 1)
                    assert step[0] == DVE_STEPS, step[0]

            def experts(b, part, n, tail=False):
                tokens = bass.ds(b * SEQ, SEQ)
                if part == "share" and n < OPEN:
                    dve.wait_ge(u_written, SETUP + u_use(b, part, n))
                    if n:
                        dve.wait_ge(xw_cut, b * OPEN + n)
                    else:
                        dve.wait_ge(h2_kept, b + 1)
                    nc.vector.tensor_tensor(xw, h2T[:, tokens], u_bank(tail, b, part, n)[0][:, 0:SEQ],
                                            ALU.mult).then_inc(u_read, 1)
                elif part == "gate":
                    dve.wait_ge(tanh_done, b * UNITS + n + 1)
                    if n >= 2:
                        dve.wait_ge(u_read, SETUP + u_use(b, "up", n - 2))
                    nc.vector.scalar_tensor_tensor(out=glu[:, n % 2, :], in0=th[:, n % 2, :], scalar=1.0,
                                                   in1=g_bank(tail, b, n)[0][:, 0:SEQ], op0=ALU.add,
                                                   op1=ALU.mult).then_inc(g_read, 1)
                elif part == "up":
                    use = u_use(b, part, n)
                    dve.wait_ge(u_written, SETUP + use)
                    dve.wait_ge(g_read, SETUP + b * UNITS + n + 1)
                    if n >= SLOTS:
                        dve.wait_ge(hid_cut, b * UNITS + n - SLOTS + 1)
                    nc.vector.tensor_tensor(hid[:, n % SLOTS, :], glu[:, n % 2, :],
                                            u_bank(tail, b, part, n)[0][:, 0:SEQ],
                                            ALU.mult).then_inc(u_read, 1)
                    if n % UP == FULL:
                        dve.wait_ge(u_read, SETUP + use)
                        dve.wait_ge(u_read, SETUP + u_use(b, "share", OPEN + n // UP))
                        nc.vector.tensor_tensor(hid[:, n % SLOTS, :], hid[:, n % SLOTS, :], pair_share,
                                                ALU.mult).then_inc(scaled, 1)
                elif part == "output":
                    dve.wait_ge(down_done, b * UNITS + UNITS)
                    nc.vector.tensor_scalar(yT, Y[:, 0:SEQ], mod[:, 5, bass.ds(b, 1)], None,
                                            ALU.mult).then_inc(y_read, 1)
                    dve.wait_ge(u_written, SETUP + u_use(b, part, n))
                    dve.wait_ge(out_free, b + 1)
                    nc.vector.tensor_tensor(y_out, x1[:, bass.ds(b * TILES, TILES), :],
                                            u_bank(tail, b, part, n)[0][:, 0:SEQ].rearrange(
                                                "p (t d) -> p t d", t=TILES), ALU.add).then_inc(u_read, 1)

            dve.wait_ge(x0_in, 16)
            run(dve, "V", attention, experts, extra={
                ("scale1",): modulate, ("scores", 0, 0): repeat_c, FOLD_AFTER: fold_gates})


_INS = ['L0_attn_h', 'L0_attn_Wqvk', 'L0_attn_Wo', 'L0_ffn_gate_w', 'L0_ffn_w1', 'L0_ffn_w2', 'L0_ffn_w3',
        'L0_c', 'L0_wmod']


def kernel(**inputs):
    import numpy as _np
    import concourse.bacc as _bacc
    from concourse import mybir as _mybir
    from concourse.bass_utils import run_bass_kernel_spmd as _run

    nc = _bacc.Bacc("TRN2", target_bir_lowering=False, num_devices=1)
    arrays, args = {}, []
    for name in _INS:
        a = _np.ascontiguousarray(inputs[name])
        arrays[f"in_{name}_dram"] = a
        args.append(nc.dram_tensor(f"in_{name}_dram", a.shape, _mybir.dt.from_np(a.dtype), kind="ExternalInput").ap())
    shape = inputs['L0_attn_h'].shape
    args.append(nc.dram_tensor("out_0_dram", shape, _mybir.dt.float32, kind="ExternalOutput").ap())
    adaln_block_kernel(nc, *args)
    r = _run(nc, [arrays], core_ids=[0])
    return r.results[0]["out_0_dram"]
```
